# Optimizing a Trainium2 kernel written in Bass

```python
import numpy as np
import jax
import jax.numpy as jnp

def _softmax(x, axis=-1):
    return jax.nn.softmax(x, axis=axis)

def _gelu(x):
    return jax.nn.gelu(x, approximate=True)

def _silu(x):
    return jax.nn.silu(x)

def _sigmoid(x):
    return jax.nn.sigmoid(x)

def _layernorm(x, axis=-1, eps=1e-05):
    m = jnp.mean(x, axis=axis, keepdims=True)
    v = jnp.var(x, axis=axis, keepdims=True)
    return (x - m) / jnp.sqrt(v + eps)

def _scatter_add(tgt, idx, src, axis=0):
    return tgt.at[idx].add(src)

def _segment_sum(src, seg, n):
    return jax.ops.segment_sum(src, seg, n)
kernel_name = 'mk_conv_preact_d2_conv_nchw256_r4_2b1e96'

def setup_inputs(seed: int=0):
    np.random.seed(seed)
    _w = jnp.asarray

    def _rec_inputs():
        import jax
        import jax.numpy as jnp
        _gk = jax.random.key(seed)
        x = -0.0002091 + 1 * jax.random.normal(jax.random.fold_in(_gk, 1), (32, 64, 56, 56), jnp.float32)
        return x
    x = _rec_inputs()

    def _L0_conv_setup():
        import jax, jax.numpy as jnp
        import numpy as np
        from jax import lax
        EPS = 1e-05

        def _prelu(x, a):
            a = a[None, :, None, None]
            return jnp.where(x >= 0, x, a * x)

        def _bn(x, gamma, beta, mean, var):
            scale = (gamma / jnp.sqrt(var + EPS))[None, :, None, None]
            shift = (beta - gamma * mean / jnp.sqrt(var + EPS))[None, :, None, None]
            return x * scale + shift
        key = jax.random.key(seed)
        ks = jax.random.split(key, 13)
        B, C, H, W = (32, 64, 56, 56)
        O = 64
        return {'x': jax.random.normal(ks[0], (B, C, H, W), jnp.float32), 'dw_weight': jax.random.normal(ks[1], (C, 1, 3, 3), jnp.float32), 'prelu1_a': jax.random.uniform(ks[2], (C,), jnp.float32) * 0.25, 'bn1_gamma': jax.random.uniform(ks[3], (C,), jnp.float32) + 0.5, 'bn1_beta': jax.random.normal(ks[4], (C,), jnp.float32) * 0.1, 'bn1_mean': jax.random.normal(ks[5], (C,), jnp.float32) * 0.1, 'bn1_var': jax.random.uniform(ks[6], (C,), jnp.float32) + 0.5, 'pw_weight': jax.random.normal(ks[7], (O, C), jnp.float32), 'prelu2_a': jax.random.uniform(ks[8], (O,), jnp.float32) * 0.25, 'bn2_gamma': jax.random.uniform(ks[9], (O,), jnp.float32) + 0.5, 'bn2_beta': jax.random.normal(ks[10], (O,), jnp.float32) * 0.1, 'bn2_mean': jax.random.normal(ks[11], (O,), jnp.float32) * 0.1, 'bn2_var': jax.random.uniform(ks[12], (O,), jnp.float32) + 0.5}
    _L0_conv_all = _L0_conv_setup()
    _L0_conv_in = {k: v for k, v in _L0_conv_all.items() if k in ('dw_weight', 'prelu1_a', 'bn1_gamma', 'bn1_beta', 'bn1_mean', 'bn1_var', 'pw_weight', 'prelu2_a', 'bn2_gamma', 'bn2_beta', 'bn2_mean', 'bn2_var')}
    del _L0_conv_all

    def _L1_conv_setup():
        import jax, jax.numpy as jnp
        import numpy as np
        K = 3
        PAD = (K - 1) // 2

        def _extract_patches(x):
            B, C, H, Wd = x.shape
            xp = jnp.pad(x, ((0, 0), (0, 0), (PAD, PAD), (PAD, PAD)))
            patches = jnp.stack([xp[:, :, i:i + H, j:j + Wd] for i in range(K) for j in range(K)], axis=-1)
            return patches
        key = jax.random.key(seed)
        k1, k2, k3 = jax.random.split(key, 3)
        B, C, H, Wd = (4, 64, 32, 32)
        x = jax.random.normal(k1, (B, C, H, Wd), dtype=jnp.float32)
        W = jax.random.normal(k2, (C * K * K, C), dtype=jnp.float32) * (1.0 / np.sqrt(C))
        b = jax.random.normal(k3, (C * K * K,), dtype=jnp.float32) * 0.01
        return {'x': x, 'W': W, 'b': b}
    _L1_conv_all = _L1_conv_setup()
    _L1_conv_in = {k: v for k, v in _L1_conv_all.items() if k in ('W', 'b')}
    del _L1_conv_all
    return {'x': x, 'L0_conv_dw_weight': _L0_conv_in['dw_weight'], 'L0_conv_prelu1_a': _L0_conv_in['prelu1_a'], 'L0_conv_bn1_gamma': _L0_conv_in['bn1_gamma'], 'L0_conv_bn1_beta': _L0_conv_in['bn1_beta'], 'L0_conv_bn1_mean': _L0_conv_in['bn1_mean'], 'L0_conv_bn1_var': _L0_conv_in['bn1_var'], 'L0_conv_pw_weight': _L0_conv_in['pw_weight'], 'L0_conv_prelu2_a': _L0_conv_in['prelu2_a'], 'L0_conv_bn2_gamma': _L0_conv_in['bn2_gamma'], 'L0_conv_bn2_beta': _L0_conv_in['bn2_beta'], 'L0_conv_bn2_mean': _L0_conv_in['bn2_mean'], 'L0_conv_bn2_var': _L0_conv_in['bn2_var'], 'L1_conv_W': _L1_conv_in['W'], 'L1_conv_b': _L1_conv_in['b']}

def reference(x, L0_conv_dw_weight, L0_conv_prelu1_a, L0_conv_bn1_gamma, L0_conv_bn1_beta, L0_conv_bn1_mean, L0_conv_bn1_var, L0_conv_pw_weight, L0_conv_prelu2_a, L0_conv_bn2_gamma, L0_conv_bn2_beta, L0_conv_bn2_mean, L0_conv_bn2_var, L1_conv_W, L1_conv_b):
    import jax
    import jax.numpy as jnp

    def _L0_conv_ref(x, dw_weight, prelu1_a, bn1_gamma, bn1_beta, bn1_mean, bn1_var, pw_weight, prelu2_a, bn2_gamma, bn2_beta, bn2_mean, bn2_var):
        import jax, jax.numpy as jnp
        import numpy as np
        from jax import lax
        EPS = 1e-05

        def _prelu(x, a):
            a = a[None, :, None, None]
            return jnp.where(x >= 0, x, a * x)

        def _bn(x, gamma, beta, mean, var):
            scale = (gamma / jnp.sqrt(var + EPS))[None, :, None, None]
            shift = (beta - gamma * mean / jnp.sqrt(var + EPS))[None, :, None, None]
            return x * scale + shift
        C = x.shape[1]
        residual = x
        h = jnp.sign(x)
        h = jnp.sign(h)
        wd = jnp.sign(dw_weight)
        h = lax.conv_general_dilated(h, wd, window_strides=(1, 1), padding=((1, 1), (1, 1)), dimension_numbers=('NCHW', 'OIHW', 'NCHW'), feature_group_count=C)
        h = _prelu(h, prelu1_a)
        h = _bn(h, bn1_gamma, bn1_beta, bn1_mean, bn1_var)
        h = jnp.sign(h)
        wp = jnp.sign(pw_weight)
        h = jnp.einsum('bchw,oc->bohw', h, wp)
        h = _prelu(h, prelu2_a)
        h = _bn(h, bn2_gamma, bn2_beta, bn2_mean, bn2_var)
        return h + residual

    def _L1_conv_ref(x, W, b):
        import jax, jax.numpy as jnp
        import numpy as np
        K = 3
        PAD = (K - 1) // 2

        def _extract_patches(x):
            B, C, H, Wd = x.shape
            xp = jnp.pad(x, ((0, 0), (0, 0), (PAD, PAD), (PAD, PAD)))
            patches = jnp.stack([xp[:, :, i:i + H, j:j + Wd] for i in range(K) for j in range(K)], axis=-1)
            return patches
        B, C, H, Wd = x.shape
        filters = jnp.einsum('bchw,oc->bohw', x, W) + b[None, :, None, None]
        filters = filters.reshape(B, C, K * K, H, Wd).transpose(0, 1, 3, 4, 2)
        patches = _extract_patches(x)
        return jnp.sum(patches * filters, axis=-1)

    def _gn(v, G=32, eps=1e-05):
        B_, C_, H_, W_ = v.shape
        g = v.reshape(B_, G, C_ // G, H_, W_)
        m = jnp.mean(g, axis=(2, 3, 4), keepdims=True)
        s = jnp.var(g, axis=(2, 3, 4), keepdims=True)
        return ((g - m) / jnp.sqrt(s + eps)).reshape(v.shape)

    def _ln_c(v, eps=1e-06):
        m = jnp.mean(v, axis=1, keepdims=True)
        s = jnp.var(v, axis=1, keepdims=True)
        return (v - m) / jnp.sqrt(s + eps)

    def _ln_t(v, eps=1e-05):
        m = jnp.mean(v, axis=-1, keepdims=True)
        s = jnp.var(v, axis=-1, keepdims=True)
        return (v - m) / jnp.sqrt(s + eps)

    def _to_tokens(v):
        B_, C_, H_, W_ = v.shape
        return v.reshape(B_, C_, H_ * W_).transpose(0, 2, 1)

    def _from_tokens(t, like):
        B_, C_, H_, W_ = like.shape
        return t.transpose(0, 2, 1).reshape(B_, C_, H_, W_)
    x = x + _L0_conv_ref(_gn(x), L0_conv_dw_weight, L0_conv_prelu1_a, L0_conv_bn1_gamma, L0_conv_bn1_beta, L0_conv_bn1_mean, L0_conv_bn1_var, L0_conv_pw_weight, L0_conv_prelu2_a, L0_conv_bn2_gamma, L0_conv_bn2_beta, L0_conv_bn2_mean, L0_conv_bn2_var)
    x = x + _L1_conv_ref(_gn(x), L1_conv_W, L1_conv_b)
    return x

_drawn_inputs = setup_inputs


def setup_inputs(seed=0):
    import zlib

    import numpy as np

    out = dict(_drawn_inputs(seed))
    spreads = {}
    factors = {'L0_conv_bn2_beta': 3.037, 'L0_conv_bn2_mean': 3.323, 'L1_conv_b': 8.0}
    for name, (base, spread) in spreads.items():
        noise = np.random.default_rng([zlib.crc32(name.encode()), seed]).standard_normal(out[name].shape)
        drawn = base * np.exp(spread * noise) if base else spread * noise
        out[name] = jnp.asarray(drawn.astype(out[name].dtype))
    for name, factor in factors.items():
        out[name] = (out[name] * factor).astype(out[name].dtype)
    return out
```

```python
from contextlib import ExitStack

import concourse.bass as bass
from concourse import mybir

F32 = mybir.dt.float32
BF16 = mybir.dt.bfloat16
FP16 = mybir.dt.float16
U32 = mybir.dt.uint32
ALU = mybir.AluOpType
ACT = mybir.ActivationFunctionType
AX = mybir.AxisListType

P = 128
RING = 4
EPS = 1e-5
G_SCALE = 2.0 ** 9
W_TOP = 2.0 ** 14


def preact_involution_kernel(nc, x, dw, a1, gam1, bet1, mu1, var1, pw, a2, gam2, bet2, mu2, var2, W, b, out):
    B, C, H, WD = x.shape
    KK = 9
    NPIX = H * WD
    TILES = B * C // P
    ROWS = 7
    CH = ROWS * WD
    CHUNKS = H // ROWS
    QUARTERS = CHUNKS // 2
    QP = 2 * CH
    QR = 2 * ROWS
    HP, WP = H + 2, WD + 2
    UNITS = QUARTERS * KK
    SLOTS = 3
    ADDS = 6
    N_GROUP = 2 * NPIX
    assert P == 2 * C and TILES % RING == 0 and UNITS % SLOTS == 0 and CH <= 512

    x_t = x.rearrange("(n s) c h w -> n (s c) (h w)", s=2)
    out_t = out.rearrange("(n s) c h w -> n (s c) (h w)", s=2)

    with ExitStack() as ctx:
        def sb(name, shape, dt):
            return ctx.enter_context(nc.sbuf_tensor(name, shape, dt))

        def sem(name):
            return ctx.enter_context(nc.semaphore(name))

        xb = sb("xb", [P, RING, NPIX], F32)
        signs = sb("signs", [P, HP, WP], BF16)
        q = sb("q", [P, 2, HP, WP], F32)
        g_hi = sb("g_hi", [P, NPIX], FP16)
        g_lo = sb("g_lo", [P, NPIX], FP16)
        stack = sb("stack", [P, 2, 2, NPIX], FP16)
        unused = sb("unused", [P, NPIX], BF16)
        ab = sb("ab", [P, 2, 2, CH], BF16)
        relu = sb("relu", [P, 2, CH], BF16)
        prod = sb("prod", [P, 2, KK, QP], F32)
        ob = sb("ob", [P, 2, QP], F32)
        st = sb("st", [P, RING, 16], F32)
        ident = sb("ident", [P, P], FP16)
        ident_bf = sb("ident_bf", [P, P], BF16)
        pw_k = sb("pw_k", [P, P], BF16)
        dw_diag = sb("dw_diag", [P, KK, P], BF16)
        pw_block = sb("pw_block", [P, P], BF16)
        pw_a = sb("pw_a", [P, P], BF16)
        pw_b = sb("pw_b", [P, P], BF16)
        w_hi = sb("w_hi", [P, KK, C], FP16)
        w_lo = sb("w_lo", [P, KK, C], FP16)
        bias = sb("bias", [P, KK], F32)
        prm = sb("prm", [P, 10], F32)
        col = sb("col", [P, 32], F32)
        minus_half = sb("minus_half", [P, 2], F32)
        st_bf = sb("st_bf", [P, 1], BF16)
        dws = sb("dws", [P, KK], F32)
        w_raw = prod[:, 0, 0, 0:KK * C]
        w_n = prod[:, 0, 1, 0:KK * C]
        dup_hi = prod[:, 0, 2, :].bitcast(FP16)[:, 0:KK * P].rearrange("p (k d i) -> p k d i", k=KK, d=2)
        dup_lo = prod[:, 0, 4, :].bitcast(FP16)[:, 0:KK * P].rearrange("p (k d i) -> p k d i", k=KK, d=2)
        pw_raw = prod[:, 0, 6, 0:C]
        dw_raw = prod[:, 0, 7, 0:KK]
        b_raw = prod[:, 0, 8, 0:KK]

        tap_ps = ctx.enter_context(nc.psum_tensor("tap_ps", [P, SLOTS, 2, 512], F32))
        dw_ps = ctx.enter_context(nc.psum_tensor("dw_ps", [P, 512], F32))
        pw_ps = ctx.enter_context(nc.psum_tensor("pw_ps", [P, 512], F32))

        A1, GAM1, BET1, MU1, VAR1, A2, GAM2, BET2, MU2, VAR2 = range(10)
        (RS1, RS2, S1, T1, S2, T2, SA, SG, TAU, NTAU, A_SC, A_BI, B_SC, B_BI, CL_A, CL_B, ST_T, C1, C2, NEG_K, Z_BI,
         WMAX, WPOW, WINV, F_UP, G_UP, G_DOWN, WSC, TMP, VE1, VE2) = range(31)
        SUM0, SH0, NM0, SQ0, SHV0, VAR0, RP0, R0, ZS, ZB = range(10)
        SUM1, NM1, SQ1, RP1, QS, QB = range(10, 16)
        SHM = sb("shm", [P, RING, 4], F32)

        def c_(n):
            return col[:, n:n + 1]

        def p_(n):
            return prm[:, n:n + 1]

        params_in, weights_in = sem("params_in"), sem("weights_in")
        ident_ready, pads_ready, half_ready = sem("ident_ready"), sem("pads_ready"), sem("half_ready")
        pool_set, dve_set, act_set = sem("pool_set"), sem("dve_set"), sem("act_set")
        var_eps_ready, rs_ready, ab_bias_ready, signs_ready = sem("var_eps_ready"), sem("rs_ready"), sem("ab_bias_ready"), sem("signs_ready")
        dup_ready, w_turned, pw_turned, k_ready, pwk_ready = sem("dup_ready"), sem("w_turned"), sem("pw_turned"), sem("k_ready"), sem("pwk_ready")
        weights_ready, consts_ready, w_copied = sem("weights_ready"), sem("consts_ready"), sem("w_copied")
        x_loaded = [sem(f"x_loaded{i}") for i in range(RING)]
        sum0_done, nm0_done, sq0_done, var0_done, r0_done = sem("sum0_done"), sem("nm0_done"), sem("sq0_done"), sem("var0_done"), sem("r0_done")
        signs_done, z_done = sem("signs_done"), sem("z_done")
        sum1_done, nm1_done, sq1_done, var1_done, r1_done = sem("sum1_done"), sem("nm1_done"), sem("sq1_done"), sem("var1_done"), sem("r1_done")
        shuffled = [sem(f"shuffled{i}") for i in range(4)]
        pow0_done, pow1_done, r0_step, r1_step = sem("pow0_done"), sem("pow1_done"), sem("r0_step"), sem("r1_step")
        q_done = sem("q_done")
        hi_done, lo_done = sem("hi_done"), sem("lo_done")
        stacked = [sem("stacked0"), sem("stacked1")]
        dw_ready, ab_done, clamped, pw_ready, relu_done, y_done, x1_done = (
            sem("dw_ready"), sem("ab_done"), sem("clamped"), sem("pw_ready"), sem("relu_done"), sem("y_done"), sem("x1_done"))
        taps_ready, prod_done, added = sem("taps_ready"), sem("prod_done"), sem("added")
        dma_added = [sem(f"dma_added{i}") for i in range(3)]
        stored = [sem("stored0"), sem("stored1")]

        def wait(eng, s, value):
            if isinstance(value, int) and value <= 0:
                return
            eng.wait_ge(s, value)

        def wait_apart(eng, s, value):
            if not isinstance(value, int):
                value = eng.to_reg(value)
                eng.wait_ge(consts_ready, 1)
            wait(eng, s, value)

        class Tile:

            def __init__(self, h, off):
                self.h, self.off = h, off
                self.slot, self.par = off % RING, off % 2

            def count(self, per, plus=0):
                return self.h * (RING * per) + (self.off * per + plus)

            def rounds(self, per=16):
                return self.h * per + (self.off // RING + 1) * per

            def index(self):
                return self.h * RING + self.off

        def program(step, loop):
            def at(h, off, first, last):
                return Tile(h, off) if first <= off <= last else None

            for i in range(-3, 1):
                step(*(Tile(0, i + d) if i + d >= 0 else None for d in range(4)))
            with loop(0, (TILES - 4) // RING) as h:
                for off in range(1, 1 + RING):
                    step(*(Tile(h, off + d) for d in range(4)))
            for i in range(TILES - 3, TILES):
                step(*(Tile(0, i + d) if i + d < TILES else None for d in range(4)))

        def rows3(ap):
            return ap.rearrange("p (a b) -> p a b", b=WD)

        block = ctx.enter_context(nc.Block())

        @block.sync
        def _(sp):
            for half in range(2):
                lo, hi = half * C, half * C + C
                for n, v in enumerate((a1, gam1, bet1, mu1, var1, a2, gam2, bet2, mu2, var2)):
                    sp.dma_start(prm[lo:hi, n:n + 1], v.rearrange("(c a) -> c a", a=1)).then_inc(params_in, 16)
                sp.dma_start(w_raw[lo:hi, :].rearrange("c (k i) -> c k i", k=KK), W.rearrange("(c k) i -> c k i", k=KK)).then_inc(weights_in, 16)
                sp.dma_start(b_raw[lo:hi, :], b.rearrange("(c k) -> c k", k=KK)).then_inc(weights_in, 16)
                sp.dma_start(dw_raw[lo:hi, :], dw.rearrange("c a i j -> c (a i j)")).then_inc(weights_in, 16)
                sp.dma_start(pw_raw[lo:hi, :], pw).then_inc(weights_in, 16)

            def store(t, qq):
                wait_apart(sp, added, t.count(4 * ADDS, ADDS * (qq + 1)))
                sp.dma_start(out_t[bass.ds(t.index(), 1), :, qq * QP:(qq + 1) * QP].rearrange("a p n -> (a p) n"),
                             ob[:, qq % 2, :]).then_inc(stored[qq % 2], 16)

            def step(taps, mid, front, load):
                if taps:
                    if not isinstance(taps.h, int) or taps.off > 0:
                        before = Tile(taps.h, taps.off - 1)
                        store(before, 1)
                        store(before, 2)
                        store(before, 3)
                if load:
                    wait_apart(sp, added, load.count(4 * ADDS, -3 * 4 * ADDS))
                    sp.dma_start(xb[:, load.slot, :],
                                 x_t[bass.ds(load.index(), 1)].rearrange("a p n -> (a p) n")).then_inc(x_loaded[load.slot], 16)
                if taps:
                    store(taps, 0)
                if mid:
                    wait_apart(sp, taps_ready, mid.count(UNITS, -UNITS))
                    for half in range(2):
                        wait_apart(sp, lo_done, mid.count(2, half + 1))
                        a, z = half * NPIX // 2, (half + 1) * NPIX // 2
                        for s in range(2):
                            own = slice(s * C, s * C + C)
                            for dst, src in ((slice(0, C), g_hi), (slice(C, P), g_lo)):
                                sp.dma_start(stack[dst, mid.par, s, a:z], src[own, a:z]).then_inc(stacked[half], 16)

            program(step, sp.Fori)
            last = Tile(0, TILES - 1)
            for qq in range(1, QUARTERS):
                store(last, qq)
            for s in stored:
                sp.wait_ge(s, 16 * 2 * TILES)

        @block.gpsimd
        def _(pool):
            pool.memset(minus_half[:], -0.5).then_inc(pool_set, 1)
            pool.memset(ident[:], 0.0).then_inc(pool_set, 1)
            pool.memset(pw_block[:], 0.0).then_inc(half_ready, 1)
            pool.wait_ge(pool_set, 2)
            pool.affine_select(out=ident[:], in_=ident[:], compare_op=ALU.not_equal, fill=1.0, base=0,
                               pattern=[[-1, P]], channel_multiplier=1).then_inc(ident_ready, 1)
            pool.memset(signs[:], 0.0).then_inc(pads_ready, 1)
            pool.wait_ge(var_eps_ready, 1)
            pool.tensor_tensor(col[:, RS1:RS2 + 1], col[:, VE1:VE2 + 1], minus_half[:], ALU.pow).then_inc(rs_ready, 1)
            pool.memset(q[:], 0.0).then_inc(pads_ready, 1)
            pool.wait_ge(consts_ready, 1)

            def s_(t, n):
                return st[:, t.slot, n:n + 1]

            def rstd0(t):
                pool.wait_ge(var0_done, t.count(1, 1))
                pool.tensor_tensor(s_(t, RP0), s_(t, VAR0), minus_half[:, 0:1], ALU.pow).then_inc(pow0_done, 1)
                wait_apart(pool, pow0_done, t.count(1, 1))
                pool.tensor_scalar(s_(t, R0), s_(t, RP0), float(N_GROUP) ** 0.5, None, ALU.mult).then_inc(r0_step, 1)
                wait_apart(pool, r0_step, t.count(1, 1))
                pool.tensor_scalar(s_(t, ZS), s_(t, R0), 1.0, None, ALU.add)
                pool.tensor_scalar(s_(t, ZB), s_(t, NM0), s_(t, R0), c_(Z_BI), ALU.mult, ALU.add).then_inc(r0_done, 1)

            def rstd1(t):
                pool.wait_ge(var1_done, t.count(1, 1))
                pool.tensor_tensor(s_(t, RP1), SHM[:, t.slot, 2:3], minus_half[:, 0:1], ALU.pow).then_inc(pow1_done, 1)
                wait_apart(pool, pow1_done, t.count(1, 1))
                pool.tensor_scalar(s_(t, QS), s_(t, RP1), c_(G_DOWN), float(N_GROUP) ** 0.5, ALU.mult, ALU.mult).then_inc(r1_step, 1)
                wait_apart(pool, r1_step, t.count(1, 1))
                pool.tensor_scalar(s_(t, QB), s_(t, NM1), s_(t, QS), None, ALU.mult).then_inc(r1_done, 1)

            def add(dst, a, c):
                return pool.tensor_tensor(dst, a, c, ALU.add).then_inc(added, 1)

            def quarter(t, qq):
                b_ = qq % 2
                pr = [prod[:, b_, k, :] for k in range(KK)]
                done = t.count(4 * ADDS, ADDS * qq)
                for m in range(3):
                    wait_apart(pool, prod_done, t.count(UNITS, KK * qq + 2 * m + 2))
                    pool.dma_start(pr[2 * m], pr[2 * m + 1], accum_op=ALU.add).then_inc(dma_added[m], 16)
                pool.wait_ge(prod_done, t.count(UNITS, KK * qq + KK))
                add(pr[6], pr[6], pr[7])
                pool.wait_ge(added, done + 1)
                add(pr[6], pr[6], pr[8])
                for m in range(3):
                    pool.wait_ge(dma_added[m], t.count(16 * 4, 16 * (qq + 1)))
                add(pr[0], pr[0], pr[2])
                pool.wait_ge(added, done + 2)
                add(pr[4], pr[4], pr[6])
                pool.wait_ge(added, done + 4)
                add(pr[0], pr[0], pr[4])
                wait(pool, stored[b_], t.count(16 * 2, 16 * (qq // 2)))
                pool.wait_ge(added, done + 5)
                add(ob[:, b_, :], pr[0], xb[:, t.slot, qq * QP:(qq + 1) * QP])

            def step(taps, mid, front, load):
                for qq in range(QUARTERS):
                    if front and qq == R0_AT:
                        rstd0(front)
                    if mid and qq == R1_AT:
                        rstd1(mid)
                    if taps:
                        quarter(taps, qq)

            program(step, pool.Fori)

        @block.tensor
        def _(pe):
            pe.wait_ge(ident_ready, 1)
            pe.wait_ge(dup_ready, 1)
            wt = [tap_ps[:, n, 0, :].bitcast(FP16)[:, 0:KK * C].rearrange("p (k c) -> p k c", k=KK) for n in range(2)]
            for n, d in enumerate((dup_hi, dup_lo)):
                for k in range(KK):
                    last = pe.transpose(wt[n][:, k, :], d[0:C, k, :, :].rearrange("p d i -> p (d i)"), ident[0:C, 0:C])
            last.then_inc(w_turned, 1)
            pe.wait_ge(signs_ready, 2)
            pe.matmul(dw_ps[:, 0:P], pw_block[:], ident_bf[:], start=True, stop=True).then_inc(pw_turned, 1)
            pe.wait_ge(pwk_ready, 1)
            pe.wait_ge(act_set, 2)
            pe.matmul(pw_ps[:, 0:1], pw_k[:], st_bf[:], start=True, stop=True).then_inc(k_ready, 1)
            pe.wait_ge(consts_ready, 1)

            def unit(t, u):
                qq, k = divmod(u, KK)
                wait(pe, prod_done, t.count(UNITS, u + 1 - SLOTS))
                for half in range(2):
                    if u == half * UNITS // 2:
                        pe.wait_ge(stacked[half], t.count(64, 64))
                for j in range(2):
                    a = (2 * qq + j) * CH
                    for w in (w_hi, w_lo):
                        for s in range(2):
                            mm = pe.matmul(tap_ps[s * C:s * C + C, u % SLOTS, j, 0:CH], w[:, k, :],
                                           stack[:, t.par, s, a:a + CH], start=(w is w_hi), stop=(w is w_lo))
                mm.then_inc(taps_ready, 1)

            def depthwise(t, c):
                if c == 0:
                    pe.wait_ge(signs_done, t.count(1, 1))
                wait(pe, ab_done, t.count(CHUNKS, c))
                for k in range(KK):
                    dy, dx = divmod(k, 3)
                    mm = pe.matmul(rows3(dw_ps[:, 0:CH]), dw_diag[:, k, :],
                                   signs[:, c * ROWS + dy:c * ROWS + dy + ROWS, dx:dx + WD],
                                   start=(k == 0), stop=(k == KK - 1))
                mm.then_inc(dw_ready, 1)

            def pointwise(t, c):
                pe.wait_ge(clamped, t.count(CHUNKS, c + 1))
                wait(pe, y_done, t.count(CHUNKS, c))
                pe.matmul(pw_ps[:, 0:CH], pw_a[:], ab[:, c % 2, 0, :], start=True, stop=False)
                pe.matmul(pw_ps[:, 0:CH], pw_b[:], ab[:, c % 2, 1, :], start=False, stop=True).then_inc(pw_ready, 1)

            def step(taps, mid, front, load):
                for u in range(UNITS):
                    if taps:
                        unit(taps, u)
                    if mid and u < CHUNKS:
                        depthwise(mid, u)
                    if mid and 0 <= u - PW_AT < CHUNKS:
                        pointwise(mid, u - PW_AT)

            program(step, pe.Fori)

        @block.scalar
        def _(act):
            def acts(o, i, f, **kw):
                return nc.scalar.activation(o, i, f, **kw)

            act.wait_ge(weights_in, 16 * 8)
            act.wait_ge(half_ready, 1)
            acts(dws[:], dw_raw, ACT.Sign).then_inc(act_set, 1)
            acts(pw_block[0:C, 0:C], pw_raw[0:C, :], ACT.Sign)
            acts(pw_block[C:P, C:P], pw_raw[C:P, :], ACT.Sign).then_inc(signs_ready, 1)
            act.wait_ge(ab_bias_ready, 1)
            acts(c_(CL_A), c_(A_BI), ACT.Sign)
            acts(c_(CL_B), c_(B_BI), ACT.Sign)
            acts(st_bf[:], c_(T1), ACT.Sign).then_inc(act_set, 1)
            act.wait_ge(consts_ready, 1)
            act.wait_ge(pads_ready, 2)

            def s_(t, n):
                return st[:, t.slot, n:n + 1]

            def conv_act(t, c):
                act.wait_ge(dw_ready, t.count(CHUNKS, c + 1))
                wait(act, pw_ready, t.count(CHUNKS, c - 1))
                acts(ab[:, c % 2, 0, :], dw_ps[:, 0:CH], ACT.Sign, scale=c_(A_SC), bias=c_(A_BI))
                acts(ab[:, c % 2, 1, :], dw_ps[:, 0:CH], ACT.Sign, scale=c_(B_SC), bias=c_(B_BI)).then_inc(ab_done, 1)

            def relu_act(t, c):
                act.wait_ge(pw_ready, t.count(CHUNKS, c + 1))
                wait(act, x1_done, t.count(CHUNKS, c - 1))
                acts(relu[:, c % 2, :], pw_ps[:, 0:CH], ACT.Relu, bias=c_(NEG_K)).then_inc(relu_done, 1)

            def sum0(t):
                act.wait_ge(x_loaded[t.slot], t.rounds())
                wait(act, sq1_done, t.count(1, -1))
                acts(unused[:], xb[:, t.slot, :], ACT.Copy, scale=-1.0 / N_GROUP, accum_out=s_(t, SUM0)).then_inc(sum0_done, 1)

            def sum1(t, front):
                act.wait_ge(x1_done, t.count(CHUNKS, CHUNKS))
                if front:
                    act.wait_ge(sum0_done, front.count(1, 1))
                else:
                    act.wait_ge(sq1_done, t.count(1, 0))
                acts(unused[:], xb[:, t.slot, :], ACT.Copy, scale=-1.0 / N_GROUP, accum_out=s_(t, SUM1)).then_inc(sum1_done, 1)

            def square0(t):
                act.wait_ge(nm0_done, t.count(1, 1))
                wait(act, sum1_done, t.count(1, 0))
                acts(unused[:], xb[:, t.slot, :], ACT.Square, bias=s_(t, NM0), accum_out=s_(t, SQ0)).then_inc(sq0_done, 1)

            def square1(t, front):
                act.wait_ge(nm1_done, t.count(1, 1))
                if front:
                    act.wait_ge(sq0_done, front.count(1, 1))
                acts(unused[:], xb[:, t.slot, :], ACT.Square, bias=s_(t, NM1), accum_out=s_(t, SQ1)).then_inc(sq1_done, 1)

            def sign0(t):
                wait(act, dw_ready, t.count(CHUNKS))
                acts(signs[:, 1:1 + H, 1:1 + WD], rows3(xb[:, t.slot, :]), ACT.Sign, bias=s_(t, NM0)).then_inc(signs_done, 1)

            def affine0(t):
                act.wait_ge(r0_done, t.count(1, 1))
                acts(xb[:, t.slot, :], xb[:, t.slot, :], ACT.Identity, scale=s_(t, ZS), bias=s_(t, ZB)).then_inc(z_done, 1)

            def q_pass(t):
                act.wait_ge(r1_done, t.count(1, 1))
                wait(act, prod_done, t.count(UNITS, -UNITS))
                acts(q[:, t.par, 1:1 + H, 1:1 + WD], rows3(xb[:, t.slot, :]), ACT.Identity,
                     scale=s_(t, QS), bias=s_(t, QB)).then_inc(q_done, 1)

            def hi_pass(t):
                act.wait_ge(q_done, t.count(1, 1))
                for half in range(2):
                    wait(act, stacked[half], t.count(64))
                    a, z = half * H // 2, (half + 1) * H // 2
                    acts(rows3(g_hi[:])[:, a:z, :], q[:, t.par, 1 + a:1 + z, 1:1 + WD], ACT.Copy,
                         scale=c_(G_UP)).then_inc(hi_done, 1)

            def step(taps, mid, front, load):
                for u in range(CHUNKS + PW_AT):
                    if mid and u < CHUNKS:
                        conv_act(mid, u)
                    if mid and u >= PW_AT:
                        relu_act(mid, u - PW_AT)
                    if front and u == SUM0_AT:
                        sum0(front)
                if mid:
                    sum1(mid, front)
                if front:
                    square0(front)
                if mid:
                    square1(mid, front)
                if front:
                    sign0(front)
                if mid:
                    q_pass(mid)
                    hi_pass(mid)
                if front:
                    affine0(front)

            program(step, act.Fori)

        @block.vector
        def _(dve):
            v = nc.vector
            steps = [0]

            def then(ins):
                steps[0] += 1
                ins.then_inc(dve_set, 1)
                dve.wait_ge(dve_set, steps[0])

            dve.wait_ge(params_in, 16 * 20)
            v.tensor_scalar(c_(VE1), p_(VAR1), EPS, None, ALU.add)
            v.tensor_scalar(c_(VE2), p_(VAR2), EPS, None, ALU.add).then_inc(var_eps_ready, 1)
            dve.wait_ge(weights_in, 16 * 8)
            then(v.tensor_reduce(c_(WMAX), w_raw, AX.X, ALU.max, apply_absolute_value=True))
            then(v.tensor_scalar(c_(WMAX), c_(WMAX), 1e-28, None, ALU.max))
            then(v.tensor_scalar(c_(WPOW).bitcast(U32), c_(WMAX).bitcast(U32), 0x7F800000, None, ALU.bitwise_and))
            then(v.reciprocal(c_(WINV), c_(WPOW)))
            then(v.tensor_scalar(c_(WSC), c_(WINV), W_TOP, None, ALU.mult))
            then(v.tensor_scalar(c_(F_UP), c_(WINV), W_TOP * G_SCALE, None, ALU.mult))
            then(v.tensor_scalar(c_(G_UP), c_(WINV), W_TOP * G_SCALE * G_SCALE, None, ALU.mult))
            then(v.tensor_scalar(c_(G_DOWN), c_(WPOW), 1.0 / (W_TOP * G_SCALE), None, ALU.mult))
            then(v.tensor_scalar(bias[:], b_raw, c_(F_UP), None, ALU.mult))
            then(v.tensor_scalar(w_n, w_raw, c_(WSC), None, ALU.mult))
            w_n3 = w_n.rearrange("p (k i) -> p k i", k=KK)
            then(v.tensor_copy(dup_hi[:, :, 0, :], w_n3))
            then(v.tensor_copy(dup_hi[:, :, 1, :], dup_hi[:, :, 0, :]))
            then(v.tensor_tensor(dup_lo[:, :, 0, :], w_n3, dup_hi[:, :, 0, :], ALU.subtract))
            v.tensor_copy(dup_lo[:, :, 1, :], dup_lo[:, :, 0, :]).then_inc(dup_ready, 1)
            dve.wait_ge(rs_ready, 1)
            for g, be, mu, rs, s, t in ((GAM1, BET1, MU1, RS1, S1, T1), (GAM2, BET2, MU2, RS2, S2, T2)):
                then(v.tensor_tensor(c_(s), p_(g), c_(rs), ALU.mult))
                then(v.tensor_tensor(c_(TMP), c_(s), p_(mu), ALU.mult))
                then(v.tensor_tensor(c_(t), p_(be), c_(TMP), ALU.subtract))
            then(v.tensor_tensor(c_(SA), c_(S1), p_(A1), ALU.mult))
            then(v.tensor_scalar(c_(SG), c_(S1), 0.0, 2.0, ALU.is_ge, ALU.mult))
            then(v.tensor_scalar(c_(SG), c_(SG), -1.0, None, ALU.add))
            then(v.tensor_scalar(c_(NTAU), c_(SA), 0.0, -2.0, ALU.is_ge, ALU.mult))
            then(v.tensor_scalar(c_(NTAU), c_(NTAU), 1.0, None, ALU.add))
            then(v.tensor_tensor(c_(A_SC), c_(S1), c_(SG), ALU.mult))
            then(v.tensor_tensor(c_(A_BI), c_(T1), c_(SG), ALU.mult))
            then(v.tensor_tensor(c_(B_SC), c_(SA), c_(NTAU), ALU.mult))
            v.tensor_tensor(c_(B_BI), c_(T1), c_(NTAU), ALU.mult).then_inc(ab_bias_ready, 1)
            then(v.tensor_tensor(c_(C1), c_(S2), p_(A2), ALU.mult))
            then(v.tensor_tensor(c_(C2), c_(S2), c_(C1), ALU.subtract))
            dve.wait_ge(ident_ready, 1)
            v.tensor_copy(ident_bf[:], ident[:]).then_inc(signs_ready, 1)
            dve.wait_ge(act_set, 1)
            for k in range(KK):
                v.tensor_scalar(dw_diag[:, k, :], ident[:], dws[:, k:k + 1], None, ALU.mult)
            dve.wait_ge(w_turned, 1)
            for n, w in enumerate((w_hi, w_lo)):
                v.tensor_copy(w[:].rearrange("p k c -> p (k c)"), tap_ps[:, n, 0, :].bitcast(FP16)[:, 0:KK * C])
            dve.wait_ge(pw_turned, 1)
            v.tensor_copy(pw_k[:], dw_ps[:, 0:P]).then_inc(pwk_ready, 1)
            v.tensor_scalar(pw_a[:], dw_ps[:, 0:P], c_(SG), None, ALU.mult)
            v.tensor_scalar(pw_b[:], dw_ps[:, 0:P], c_(NTAU), None, ALU.mult)
            dve.wait_ge(k_ready, 1)
            then(v.tensor_scalar(c_(NEG_K), pw_ps[:, 0:1], -1.0, None, ALU.mult))
            then(v.tensor_tensor(c_(TMP), c_(NEG_K), c_(C1), ALU.mult))
            dve.wait_ge(act_set, 2)
            v.tensor_tensor(c_(Z_BI), c_(T2), c_(TMP), ALU.add).then_inc(consts_ready, 1)
            dve.wait_ge(consts_ready, 1)
            dve.wait_ge(pads_ready, 2)

            def s_(t, n):
                return st[:, t.slot, n:n + 1]

            PAIR = [i ^ 1 for i in range(32)]

            def pair_sum(t, src, tmp, shuf, dst, ready, done, extra):
                wait_apart(dve, ready, t.count(1, 1))
                v.stream_shuffle(tmp, src, PAIR).then_inc(shuf, 1)
                dve.wait_ge(shuf, t.count(1, 1))
                v.tensor_scalar(dst, src, tmp, extra, ALU.add, ALU.add).then_inc(done, 1)

            def mean0(t):
                pair_sum(t, s_(t, SUM0), s_(t, SH0), shuffled[0], s_(t, NM0), sum0_done, nm0_done, 0.0)

            def var0(t):
                pair_sum(t, s_(t, SQ0), s_(t, SHV0), shuffled[1], s_(t, VAR0), sq0_done, var0_done, EPS * N_GROUP)

            def mean1(t):
                pair_sum(t, s_(t, SUM1), SHM[:, t.slot, 0:1], shuffled[2], s_(t, NM1), sum1_done, nm1_done, 0.0)

            def var1(t):
                pair_sum(t, s_(t, SQ1), SHM[:, t.slot, 1:2], shuffled[3], SHM[:, t.slot, 2:3], sq1_done, var1_done, EPS * N_GROUP)

            def clamp(t, c):
                dve.wait_ge(ab_done, t.count(CHUNKS, c + 1))
                v.tensor_scalar(ab[:, c % 2, 0, :], ab[:, c % 2, 0, :], c_(CL_A), None, ALU.max)
                v.tensor_scalar(ab[:, c % 2, 1, :], ab[:, c % 2, 1, :], c_(CL_B), None, ALU.max).then_inc(clamped, 1)

            def x1_linear(t, c):
                if c == 0:
                    dve.wait_ge(z_done, t.count(1, 1))
                dve.wait_ge(relu_done, t.count(CHUNKS, c + 1))
                xc = xb[:, t.slot, c * CH:(c + 1) * CH]
                v.scalar_tensor_tensor(xc, pw_ps[:, 0:CH], c_(C1), xc, ALU.mult, ALU.add).then_inc(y_done, 1)

            def x1_relu(t, c):
                dve.wait_ge(y_done, t.count(CHUNKS, c + 1))
                xc = xb[:, t.slot, c * CH:(c + 1) * CH]
                v.scalar_tensor_tensor(xc, relu[:, c % 2, :], c_(C2), xc, ALU.mult, ALU.add).then_inc(x1_done, 1)

            def low(t, half):
                dve.wait_ge(hi_done, t.count(2, half + 1))
                wait(dve, stacked[half], t.count(64))
                a, z = half * H // 2, (half + 1) * H // 2
                v.scalar_tensor_tensor(rows3(g_lo[:])[:, a:z, :], q[:, t.par, 1 + a:1 + z, 1:1 + WD], c_(G_UP),
                                       rows3(g_hi[:])[:, a:z, :], ALU.mult, ALU.subtract).then_inc(lo_done, 1)

            FREED = {7: 1, 8: 2, 1: 3, 2: 3, 3: 3, 5: 3, 6: 4, 4: 5, 0: 6}

            def product(t, u):
                qq, k = divmod(u, KK)
                dy, dx = divmod(k, 3)
                if u == 0:
                    dve.wait_ge(q_done, t.count(1, 1))
                wait(dve, added, t.count(4 * ADDS, ADDS * (qq - 2) + FREED[k]))
                dve.wait_ge(taps_ready, t.count(UNITS, u + 1))
                r = qq * QR + dy
                v.scalar_tensor_tensor(
                    prod[:, qq % 2, k, :].rearrange("p (j a b) -> p j a b", j=2, b=WD),
                    tap_ps[:, u % SLOTS, :, 0:CH].rearrange("p j (a b) -> p j a b", b=WD), bias[:, k:k + 1],
                    q[:, t.par, r:r + QR, dx:dx + WD].rearrange("p (j a) b -> p j a b", j=2),
                    ALU.add, ALU.mult).then_inc(prod_done, 1)

            def step(taps, mid, front, load):
                for u in range(UNITS):
                    if mid and 0 <= u - CLAMP_AT < CHUNKS:
                        clamp(mid, u - CLAMP_AT)
                    if mid and 0 <= u - X1_AT < CHUNKS:
                        x1_linear(mid, u - X1_AT)
                    if taps:
                        product(taps, u)
                    if mid and 0 <= u - X1_AT < CHUNKS:
                        x1_relu(mid, u - X1_AT)
                    for at, who, what in ((MEAN1_AT, mid, mean1), (VAR1_AT, mid, var1), (MEAN0_AT, front, mean0),
                                          (VAR0_AT, front, var0)):
                        if u == at and who:
                            what(who)
                    for half in range(2):
                        if mid and u == LOW_AT[half]:
                            low(mid, half)

            program(step, dve.Fori)


PW_AT = 2
CLAMP_AT = 1
X1_AT = 3
SUM0_AT = 4
MEAN0_AT = 7
MEAN1_AT = 14
VAR0_AT = 17
VAR1_AT = 20
R0_AT = 1
R1_AT = 1
LOW_AT = (31, 33)

_INS = ["x", "L0_conv_dw_weight", "L0_conv_prelu1_a", "L0_conv_bn1_gamma", "L0_conv_bn1_beta", "L0_conv_bn1_mean",
        "L0_conv_bn1_var", "L0_conv_pw_weight", "L0_conv_prelu2_a", "L0_conv_bn2_gamma", "L0_conv_bn2_beta",
        "L0_conv_bn2_mean", "L0_conv_bn2_var", "L1_conv_W", "L1_conv_b"]


def kernel(**inputs):
    import numpy as _np
    import concourse.bacc as _bacc
    from concourse import mybir as _mybir
    from concourse.bass_utils import run_bass_kernel_spmd as _run

    nc = _bacc.Bacc("TRN2", target_bir_lowering=False, num_devices=1)
    arrays, args = {}, []
    for name in _INS:
        a = _np.ascontiguousarray(inputs[name])
        arrays[f"in_{name}_dram"] = a
        args.append(nc.dram_tensor(f"in_{name}_dram", a.shape, _mybir.dt.from_np(a.dtype), kind="ExternalInput").ap())
    shape = inputs["x"].shape
    args.append(nc.dram_tensor("out_0_dram", shape, _mybir.dt.from_np(_np.dtype("float32")), kind="ExternalOutput").ap())
    preact_involution_kernel(nc, *args)
    r = _run(nc, [arrays], core_ids=[0])
    return r.results[0]["out_0_dram"]
```

```python
from contextlib import ExitStack

import concourse.bass as bass
from concourse import mybir

F32 = mybir.dt.float32
BF16 = mybir.dt.bfloat16
FP16 = mybir.dt.float16
U32 = mybir.dt.uint32
ALU = mybir.AluOpType
ACT = mybir.ActivationFunctionType
AX = mybir.AxisListType

P = 128
RING = 4
EPS = 1e-5
G_SCALE = 2.0 ** 9
W_TOP = 2.0 ** 14


def preact_involution_kernel(nc, x, dw, a1, gam1, bet1, mu1, var1, pw, a2, gam2, bet2, mu2, var2, W, b, out):
    B, C, H, WD = x.shape
    KK = 9
    NPIX = H * WD
    TILES = B * C // P
    ROWS = 7
    CH = ROWS * WD
    CHUNKS = H // ROWS
    QUARTERS = CHUNKS // 2
    QP = 2 * CH
    QR = 2 * ROWS
    HP, WP = H + 2, WD + 2
    UNITS = QUARTERS * KK
    SLOTS = 3
    ADDS = 4
    N_GROUP = 2 * NPIX
    assert P == 2 * C and TILES % RING == 0 and UNITS % SLOTS == 0 and CH <= 512

    x_t = x.rearrange("(n s) c h w -> n (s c) (h w)", s=2)
    out_t = out.rearrange("(n s) c h w -> n (s c) (h w)", s=2)

    with ExitStack() as ctx:
        def sb(name, shape, dt):
            return ctx.enter_context(nc.sbuf_tensor(name, shape, dt))

        def sem(name):
            return ctx.enter_context(nc.semaphore(name))

        xb = sb("xb", [P, RING, NPIX], F32)
        signs = sb("signs", [P, HP, WP], BF16)
        q = sb("q", [P, 2, HP, WP], F32)
        g_hi = sb("g_hi", [P, NPIX], FP16)
        g_lo = sb("g_lo", [P, NPIX], FP16)
        stack = sb("stack", [P, 2, 2, NPIX], FP16)
        unused = sb("unused", [P, NPIX], BF16)
        ab = sb("ab", [P, 2, 2, CH], BF16)
        relu = sb("relu", [P, 2, CH], F32)
        prod = sb("prod", [P, 2, KK, QP], F32)
        ob = sb("ob", [P, 2, QP], F32)
        st = sb("st", [P, RING, 19], F32)
        ident = sb("ident", [P, P], FP16)
        ident_bf = sb("ident_bf", [P, P], BF16)
        pw_k = sb("pw_k", [P, P], BF16)
        dw_diag = sb("dw_diag", [P, KK, P], BF16)
        pw_block = sb("pw_block", [P, P], BF16)
        pw_a = sb("pw_a", [P, P], BF16)
        pw_b = sb("pw_b", [P, P], BF16)
        w_hi = sb("w_hi", [P, KK, C], FP16)
        w_lo = sb("w_lo", [P, KK, C], FP16)
        bias = sb("bias", [P, KK], F32)
        prm = sb("prm", [P, 10], F32)
        col = sb("col", [P, 40], F32)
        minus_half = sb("minus_half", [P, 2], F32)
        st_bf = sb("st_bf", [P, 1], BF16)
        dws = sb("dws", [P, KK], F32)
        w_raw = prod[:, 0, 0, 0:KK * C]
        w_n = prod[:, 0, 1, 0:KK * C]
        dup_hi = prod[:, 0, 2, :].bitcast(FP16)[:, 0:KK * P].rearrange("p (k d i) -> p k d i", k=KK, d=2)
        dup_lo = prod[:, 0, 4, :].bitcast(FP16)[:, 0:KK * P].rearrange("p (k d i) -> p k d i", k=KK, d=2)
        pw_raw = prod[:, 0, 6, 0:C]
        dw_raw = prod[:, 0, 7, 0:KK]
        b_raw = prod[:, 0, 8, 0:KK]

        tap_ps = ctx.enter_context(nc.psum_tensor("tap_ps", [P, SLOTS, 2, 512], F32))
        dw_ps = ctx.enter_context(nc.psum_tensor("dw_ps", [P, 512], F32))
        pw_ps = ctx.enter_context(nc.psum_tensor("pw_ps", [P, 512], F32))

        A1, GAM1, BET1, MU1, VAR1, A2, GAM2, BET2, MU2, VAR2 = range(10)
        (RS1, RS2, S1, T1, S2, T2, SA, SG, TAU, NTAU, A_SC, A_BI, B_SC, B_BI, CL_A, CL_B, ST_T, C1, C2, NEG_K, Z_BI,
         WMAX, WPOW, WINV, F_UP, G_UP, G_DOWN, WSC, TMP, VE1, VE2, SG2, C2_ABS, C1_SG, NEG_KC, Z_BI_SG, MEAN_SG) = range(37)
        SUM0, SH0, NM0, SQ0, SHV0, VAR0, RP0, R0, ZS, ZB = range(10)
        SUM1, NM1, SQ1, RP1, QS, QB, B4, QS_SG, MEAN1 = range(10, 19)
        SHM = sb("shm", [P, RING, 4], F32)

        def c_(n):
            return col[:, n:n + 1]

        def p_(n):
            return prm[:, n:n + 1]

        params_in, weights_in = sem("params_in"), sem("weights_in")
        ident_ready, pads_ready, half_ready = sem("ident_ready"), sem("pads_ready"), sem("half_ready")
        pool_set, dve_set, act_set = sem("pool_set"), sem("dve_set"), sem("act_set")
        var_eps_ready, rs_ready, ab_bias_ready, signs_ready = sem("var_eps_ready"), sem("rs_ready"), sem("ab_bias_ready"), sem("signs_ready")
        dup_ready, w_turned, pw_turned, k_ready, pwk_ready = sem("dup_ready"), sem("w_turned"), sem("pw_turned"), sem("k_ready"), sem("pwk_ready")
        weights_ready, consts_ready, w_copied = sem("weights_ready"), sem("consts_ready"), sem("w_copied")
        x_loaded = [sem(f"x_loaded{i}") for i in range(RING)]
        sum0_done, nm0_done, sq0_done, var0_done, r0_done = sem("sum0_done"), sem("nm0_done"), sem("sq0_done"), sem("var0_done"), sem("r0_done")
        signs_done, z_done = sem("signs_done"), sem("z_done")
        sum1_done, nm1_done, sq1_done, var1_done, r1_done = sem("sum1_done"), sem("nm1_done"), sem("sq1_done"), sem("var1_done"), sem("r1_done")
        shuffled = [sem(f"shuffled{i}") for i in range(4)]
        pow0_done, pow1_done, r0_step, r1_step = sem("pow0_done"), sem("pow1_done"), sem("r0_step"), sem("r1_step")
        q_done, inverse_done, b4_done = sem("q_done"), sem("inverse_done"), sem("b4_done")
        hi_done, lo_done = sem("hi_done"), sem("lo_done")
        stacked = [sem("stacked0"), sem("stacked1")]
        dw_ready, ab_done, clamped, pw_ready, relu_done, y_done, x1_done = (
            sem("dw_ready"), sem("ab_done"), sem("clamped"), sem("pw_ready"), sem("relu_done"), sem("y_done"), sem("x1_done"))
        taps_ready, prod_done, added = sem("taps_ready"), sem("prod_done"), sem("added")
        folded, mean_added = sem("folded"), sem("mean_added")
        stored = [sem("stored0"), sem("stored1")]

        def wait(eng, s, value):
            if isinstance(value, int) and value <= 0:
                return
            eng.wait_ge(s, value)

        def wait_apart(eng, s, value):
            if not isinstance(value, int):
                value = eng.to_reg(value)
                eng.wait_ge(consts_ready, 1)
            wait(eng, s, value)

        class Tile:

            def __init__(self, h, off):
                self.h, self.off = h, off
                self.slot, self.par = off % RING, off % 2

            def count(self, per, plus=0):
                assert isinstance(self.h, int) or self.off * per + plus > 0
                return self.h * (RING * per) + (self.off * per + plus)

            def rounds(self, per=16):
                return self.h * per + (self.off // RING + 1) * per

            def index(self):
                return self.h * RING + self.off

        def program(step, loop):
            def peeled(i):
                step(*(Tile(0, i + d) if 0 <= i + d < TILES else None for d in range(-1, 4)))

            for i in range(-3, 1):
                peeled(i)
            with loop(0, (TILES - 4) // RING) as h:
                for off in range(1, 1 + RING):
                    step(*(Tile(h, off + d) for d in range(-1, 4)))
            for i in range(TILES - 3, TILES + 1):
                peeled(i)

        def due(u, delay, first, every, count, now, later):
            for piece in range(count):
                at = first + every * piece + delay
                tile = now if at < UNITS else later
                if tile and at % UNITS == u:
                    yield tile, piece

        def chunks_due(u, delay, mid, front):
            return due(u, delay, FIRST_CHUNK, CHUNK_EVERY, CHUNKS, front, mid)

        def quarters_due(u, delay, done, taps):
            return due(u, delay, KK, KK, QUARTERS, taps, done)

        def rows3(ap):
            return ap.rearrange("p (a b) -> p a b", b=WD)

        block = ctx.enter_context(nc.Block())

        @block.sync
        def _(sp):
            for half in range(2):
                lo, hi = half * C, half * C + C
                for n, v in enumerate((a1, gam1, bet1, mu1, var1, a2, gam2, bet2, mu2, var2)):
                    sp.dma_start(prm[lo:hi, n:n + 1], v.rearrange("(c a) -> c a", a=1)).then_inc(params_in, 16)
                sp.dma_start(w_raw[lo:hi, :].rearrange("c (k i) -> c k i", k=KK), W.rearrange("(c k) i -> c k i", k=KK)).then_inc(weights_in, 16)
                sp.dma_start(b_raw[lo:hi, :], b.rearrange("(c k) -> c k", k=KK)).then_inc(weights_in, 16)
                sp.dma_start(dw_raw[lo:hi, :], dw.rearrange("c a i j -> c (a i j)")).then_inc(weights_in, 16)
                sp.dma_start(pw_raw[lo:hi, :], pw).then_inc(weights_in, 16)

            def store(t, qq):
                wait_apart(sp, added, t.count(4 * ADDS, ADDS * (qq + 1)))
                sp.dma_start(out_t[bass.ds(t.index(), 1), :, qq * QP:(qq + 1) * QP].rearrange("a p n -> (a p) n"),
                             ob[:, qq % 2, :]).then_inc(stored[qq % 2], 16)

            def stack_half(t, half):
                wait_apart(sp, lo_done, t.count(2, half + 1))
                a, z = half * NPIX // 2, (half + 1) * NPIX // 2
                for s in range(2):
                    own = slice(s * C, s * C + C)
                    for dst, src in ((slice(0, C), g_hi), (slice(C, P), g_lo)):
                        sp.dma_start(stack[dst, t.par, s, a:z], src[own, a:z]).then_inc(stacked[half], 16)

            def step(done, taps, mid, front, load):
                if load:
                    wait_apart(sp, q_done, load.count(1, -3))
                    sp.dma_start(xb[:, load.slot, :],
                                 x_t[bass.ds(load.index(), 1)].rearrange("a p n -> (a p) n")).then_inc(x_loaded[load.slot], 16)
                for u in range(UNITS):
                    for t, qq in quarters_due(u, OUT_DELAY + 1, done, taps):
                        store(t, qq)
                    for half in range(2):
                        if mid and u == LOW_AT[half] + 1:
                            if half == 0:
                                wait_apart(sp, taps_ready, mid.count(UNITS, -UNITS))
                            stack_half(mid, half)

            program(step, sp.Fori)
            for s in stored:
                sp.wait_ge(s, 16 * 2 * TILES)

        @block.gpsimd
        def _(pool):
            pool.memset(minus_half[:], -0.5).then_inc(pool_set, 1)
            pool.memset(ident[:], 0.0).then_inc(pool_set, 1)
            pool.memset(pw_block[:], 0.0).then_inc(half_ready, 1)
            pool.wait_ge(pool_set, 2)
            pool.affine_select(out=ident[:], in_=ident[:], compare_op=ALU.not_equal, fill=1.0, base=0,
                               pattern=[[-1, P]], channel_multiplier=1).then_inc(ident_ready, 1)
            pool.memset(signs[:], 0.0).then_inc(pads_ready, 1)
            pool.wait_ge(var_eps_ready, 1)
            pool.tensor_tensor(col[:, RS1:RS2 + 1], col[:, VE1:VE2 + 1], minus_half[:], ALU.pow).then_inc(rs_ready, 1)
            pool.memset(q[:], 0.0).then_inc(pads_ready, 1)
            pool.wait_ge(consts_ready, 1)

            def s_(t, n):
                return st[:, t.slot, n:n + 1]

            def rstd0(t):
                pool.wait_ge(var0_done, t.count(1, 1))
                pool.tensor_tensor(s_(t, RP0), s_(t, VAR0), minus_half[:, 0:1], ALU.pow).then_inc(pow0_done, 1)
                wait_apart(pool, pow0_done, t.count(1, 1))
                pool.tensor_scalar(s_(t, R0), s_(t, RP0), c_(SG2), float(N_GROUP) ** 0.5, ALU.mult, ALU.mult).then_inc(r0_step, 1)
                wait_apart(pool, r0_step, t.count(1, 1))
                pool.tensor_scalar(s_(t, ZS), s_(t, R0), c_(SG2), None, ALU.add)
                pool.tensor_scalar(s_(t, ZB), s_(t, NM0), s_(t, R0), c_(Z_BI_SG), ALU.mult, ALU.add).then_inc(r0_done, 1)

            def rstd1(t):
                pool.wait_ge(var1_done, t.count(1, 1))
                pool.tensor_tensor(s_(t, RP1), SHM[:, t.slot, 2:3], minus_half[:, 0:1], ALU.pow).then_inc(pow1_done, 1)
                wait_apart(pool, pow1_done, t.count(1, 1))
                pool.tensor_scalar(s_(t, QS), s_(t, RP1), c_(G_DOWN), float(N_GROUP) ** 0.5, ALU.mult, ALU.mult).then_inc(r1_step, 1)
                wait_apart(pool, r1_step, t.count(1, 1))
                pool.tensor_scalar(s_(t, MEAN1), s_(t, NM1), -1.0, None, ALU.mult)
                pool.tensor_scalar(s_(t, QS_SG), s_(t, QS), c_(SG2), None, ALU.mult)
                pool.tensor_scalar(s_(t, QB), s_(t, NM1), s_(t, QS), None, ALU.mult).then_inc(r1_done, 1)

            def add(dst, a, c):
                return pool.tensor_tensor(dst, a, c, ALU.add).then_inc(added, 1)

            def products(qq):
                return [prod[:, qq % 2, n, :] for n in range(KK)]

            def fold(t, qq):
                wait_apart(pool, prod_done, t.count(UNITS, KK * qq + KK - 1))
                pool.dma_start(prod[:, qq % 2, 0:4, :], prod[:, qq % 2, 4:8, :], accum_op=ALU.add,
                               max_dma_last_dim=2 * QP).then_inc(folded, 16)

            def add23(t, qq):
                pr = products(qq)
                pool.wait_ge(folded, t.count(16 * 4, 16 * (qq + 1)))
                add(pr[2], pr[2], pr[3])

            def add01(t, qq):
                pr = products(qq)
                add(pr[0], pr[0], pr[1])

            def add02(t, qq):
                pr = products(qq)
                pool.wait_ge(added, t.count(4 * ADDS, ADDS * qq + 2))
                add(pr[0], pr[0], pr[2])

            def final(t, qq):
                pr = products(qq)
                wait_apart(pool, mean_added, t.count(4, qq + 1))
                wait_apart(pool, stored[qq % 2], t.count(16 * 2, 16 * (qq // 2)))
                wait_apart(pool, added, t.count(4 * ADDS, ADDS * qq + 3))
                add(ob[:, qq % 2, :], pr[8], pr[0])

            def x1_relu(t, c):
                wait_apart(pool, relu_done, t.count(CHUNKS, c + 1))
                wait_apart(pool, y_done, t.count(CHUNKS, c + 1))
                xc = xb[:, t.slot, c * CH:(c + 1) * CH]
                pool.tensor_tensor(xc, xc, relu[:, c % 2, :], ALU.add).then_inc(x1_done, 1)

            def step(done, taps, mid, front, load):
                for u in range(UNITS):
                    for what, delay in ((fold, 0), (add23, ADD_DELAY), (add01, ADD_DELAY + 1), (add02, ADD_DELAY + 3),
                                        (final, OUT_DELAY)):
                        for t, qq in quarters_due(u, delay, done, taps):
                            what(t, qq)
                    for t, c in chunks_due(u, X1_DELAY + 1, mid, front):
                        x1_relu(t, c)
                    if front and u == R0_AT:
                        rstd0(front)
                    if mid and u == R1_AT:
                        rstd1(mid)

            program(step, pool.Fori)

        @block.tensor
        def _(pe):
            pe.wait_ge(ident_ready, 1)
            pe.wait_ge(dup_ready, 1)
            wt = [tap_ps[:, n, 0, :].bitcast(FP16)[:, 0:KK * C].rearrange("p (k c) -> p k c", k=KK) for n in range(2)]
            for n, d in enumerate((dup_hi, dup_lo)):
                for k in range(KK):
                    last = pe.transpose(wt[n][:, k, :], d[0:C, k, :, :].rearrange("p d i -> p (d i)"), ident[0:C, 0:C])
            last.then_inc(w_turned, 1)
            pe.wait_ge(signs_ready, 2)
            pe.matmul(dw_ps[:, 0:P], pw_block[:], ident_bf[:], start=True, stop=True).then_inc(pw_turned, 1)
            pe.wait_ge(pwk_ready, 1)
            pe.wait_ge(act_set, 2)
            pe.matmul(pw_ps[:, 0:1], pw_k[:], st_bf[:], start=True, stop=True).then_inc(k_ready, 1)
            pe.wait_ge(consts_ready, 1)

            def unit(t, u):
                qq, k = divmod(u, KK)
                wait(pe, prod_done, t.count(UNITS, u + 1 - SLOTS))
                for half in range(2):
                    if u == half * UNITS // 2:
                        pe.wait_ge(stacked[half], t.count(64, 64))
                for j in range(2):
                    a = (2 * qq + j) * CH
                    for w in (w_hi, w_lo):
                        for s in range(2):
                            mm = pe.matmul(tap_ps[s * C:s * C + C, u % SLOTS, j, 0:CH], w[:, k, :],
                                           stack[:, t.par, s, a:a + CH], start=(w is w_hi), stop=(w is w_lo))
                mm.then_inc(taps_ready, 1)

            def depthwise(t, c, taps):
                if c == 0 and taps.start == 0:
                    pe.wait_ge(signs_done, t.count(1, 1))
                if taps.start == 0:
                    wait(pe, ab_done, t.count(CHUNKS, c))
                for k in taps:
                    dy, dx = divmod(k, 3)
                    mm = pe.matmul(rows3(dw_ps[:, 0:CH]), dw_diag[:, k, :],
                                   signs[:, c * ROWS + dy:c * ROWS + dy + ROWS, dx:dx + WD],
                                   start=(k == 0), stop=(k == KK - 1))
                if taps.stop == KK:
                    mm.then_inc(dw_ready, 1)

            def pointwise(t, c):
                pe.wait_ge(clamped, t.count(CHUNKS, c + 1))
                wait(pe, y_done, t.count(CHUNKS, c))
                pe.matmul(pw_ps[:, 0:CH], pw_a[:], ab[:, c % 2, 0, :], start=True, stop=False)
                pe.matmul(pw_ps[:, 0:CH], pw_b[:], ab[:, c % 2, 1, :], start=False, stop=True).then_inc(pw_ready, 1)

            def step(done, taps, mid, front, load):
                for u in range(UNITS):
                    if taps:
                        unit(taps, u)
                    for t, c in chunks_due(u, 0, mid, front):
                        depthwise(t, c, range(0, 5))
                    for t, c in chunks_due(u, 1, mid, front):
                        depthwise(t, c, range(5, KK))
                    for t, c in chunks_due(u, PW_DELAY, mid, front):
                        pointwise(t, c)

            program(step, pe.Fori)

        @block.scalar
        def _(act):
            def acts(o, i, f, **kw):
                return nc.scalar.activation(o, i, f, **kw)

            act.wait_ge(weights_in, 16 * 8)
            act.wait_ge(half_ready, 1)
            acts(dws[:], dw_raw, ACT.Sign).then_inc(act_set, 1)
            acts(pw_block[0:C, 0:C], pw_raw[0:C, :], ACT.Sign)
            acts(pw_block[C:P, C:P], pw_raw[C:P, :], ACT.Sign).then_inc(signs_ready, 1)
            act.wait_ge(ab_bias_ready, 1)
            acts(c_(CL_A), c_(A_BI), ACT.Sign)
            acts(c_(CL_B), c_(B_BI), ACT.Sign)
            acts(st_bf[:], c_(T1), ACT.Sign).then_inc(act_set, 1)
            act.wait_ge(consts_ready, 1)
            act.wait_ge(pads_ready, 2)

            def s_(t, n):
                return st[:, t.slot, n:n + 1]

            def conv_act(t, c):
                act.wait_ge(dw_ready, t.count(CHUNKS, c + 1))
                wait(act, pw_ready, t.count(CHUNKS, c - 1))
                acts(ab[:, c % 2, 0, :], dw_ps[:, 0:CH], ACT.Sign, scale=c_(A_SC), bias=c_(A_BI))
                acts(ab[:, c % 2, 1, :], dw_ps[:, 0:CH], ACT.Sign, scale=c_(B_SC), bias=c_(B_BI)).then_inc(ab_done, 1)

            def relu_act(t, c):
                act.wait_ge(pw_ready, t.count(CHUNKS, c + 1))
                wait(act, x1_done, t.count(CHUNKS, c - 1))
                acts(relu[:, c % 2, :], pw_ps[:, 0:CH], ACT.Relu, scale=c_(C2_ABS), bias=c_(NEG_KC)).then_inc(relu_done, 1)

            def sum0(t):
                act.wait_ge(x_loaded[t.slot], t.rounds())
                wait(act, sq1_done, t.count(1, -1))
                acts(unused[:], xb[:, t.slot, :], ACT.Copy, scale=-1.0 / N_GROUP, accum_out=s_(t, SUM0)).then_inc(sum0_done, 1)

            def sum1(t, front):
                act.wait_ge(x1_done, t.count(CHUNKS, CHUNKS))
                if front:
                    act.wait_ge(sq0_done, front.count(1, 1))
                else:
                    act.wait_ge(sq1_done, t.count(1, 0))
                acts(unused[:], xb[:, t.slot, :], ACT.Copy, scale=c_(MEAN_SG), accum_out=s_(t, SUM1)).then_inc(sum1_done, 1)

            def square0(t):
                act.wait_ge(nm0_done, t.count(1, 1))
                acts(unused[:], xb[:, t.slot, :], ACT.Square, bias=s_(t, NM0), accum_out=s_(t, SQ0)).then_inc(sq0_done, 1)

            def square1(t):
                act.wait_ge(nm1_done, t.count(1, 1))
                acts(unused[:], xb[:, t.slot, :], ACT.Square, scale=c_(SG2), bias=s_(t, NM1), accum_out=s_(t, SQ1)).then_inc(sq1_done, 1)

            def sign0(t):
                wait(act, dw_ready, t.count(CHUNKS))
                acts(signs[:, 1:1 + H, 1:1 + WD], rows3(xb[:, t.slot, :]), ACT.Sign, bias=s_(t, NM0)).then_inc(signs_done, 1)

            def affine0(t):
                act.wait_ge(r0_done, t.count(1, 1))
                acts(xb[:, t.slot, :], xb[:, t.slot, :], ACT.Identity, scale=s_(t, ZS), bias=s_(t, ZB)).then_inc(z_done, 1)

            def q_pass(t):
                act.wait_ge(r1_done, t.count(1, 1))
                wait(act, prod_done, t.count(UNITS, -UNITS))
                acts(q[:, t.par, 1:1 + H, 1:1 + WD], rows3(xb[:, t.slot, :]), ACT.Identity,
                     scale=s_(t, QS_SG), bias=s_(t, QB)).then_inc(q_done, 1)

            def hi_half(t, half):
                act.wait_ge(q_done, t.count(1, 1))
                wait(act, stacked[half], t.count(64))
                a, z = half * H // 2, (half + 1) * H // 2
                acts(rows3(g_hi[:])[:, a:z, :], q[:, t.par, 1 + a:1 + z, 1:1 + WD], ACT.Copy,
                     scale=c_(G_UP)).then_inc(hi_done, 1)

            def add_mean(t, qq):
                act.wait_ge(prod_done, t.count(UNITS, KK * qq + KK))
                acts(prod[:, qq % 2, 8, :], prod[:, qq % 2, 8, :], ACT.Identity, bias=s_(t, MEAN1)).then_inc(mean_added, 1)

            def step(done, taps, mid, front, load):
                for u in range(UNITS):
                    for t, qq in quarters_due(u, MEAN_DELAY, done, taps):
                        add_mean(t, qq)
                    for t, c in chunks_due(u, 1, mid, front):
                        conv_act(t, c)
                    for t, c in chunks_due(u, PW_DELAY, mid, front):
                        relu_act(t, c)
                    if front:
                        for at, what in ((SUM0_AT, sum0), (SQUARE0_AT, square0), (SIGN0_AT, sign0), (AFFINE0_AT, affine0)):
                            if u == at:
                                what(front)
                    if mid and u == SUM1_AT:
                        sum1(mid, front)
                    if mid and u == SQUARE1_AT:
                        square1(mid)
                    if mid and u == Q_AT:
                        q_pass(mid)
                    for half in range(2):
                        if mid and u == HI_AT[half]:
                            hi_half(mid, half)

            program(step, act.Fori)

        @block.vector
        def _(dve):
            v = nc.vector
            steps = [0]

            def then(ins):
                steps[0] += 1
                ins.then_inc(dve_set, 1)
                dve.wait_ge(dve_set, steps[0])

            dve.wait_ge(params_in, 16 * 20)
            v.tensor_scalar(c_(VE1), p_(VAR1), EPS, None, ALU.add)
            v.tensor_scalar(c_(VE2), p_(VAR2), EPS, None, ALU.add).then_inc(var_eps_ready, 1)
            dve.wait_ge(weights_in, 16 * 8)
            then(v.tensor_reduce(c_(WMAX), w_raw, AX.X, ALU.max, apply_absolute_value=True))
            then(v.tensor_scalar(c_(WMAX), c_(WMAX), 1e-28, None, ALU.max))
            then(v.tensor_scalar(c_(WPOW).bitcast(U32), c_(WMAX).bitcast(U32), 0x7F800000, None, ALU.bitwise_and))
            then(v.reciprocal(c_(WINV), c_(WPOW)))
            then(v.tensor_scalar(c_(WSC), c_(WINV), W_TOP, None, ALU.mult))
            then(v.tensor_scalar(c_(F_UP), c_(WINV), W_TOP * G_SCALE, None, ALU.mult))
            then(v.tensor_scalar(c_(G_UP), c_(WINV), W_TOP * G_SCALE * G_SCALE, None, ALU.mult))
            then(v.tensor_scalar(c_(G_DOWN), c_(WPOW), 1.0 / (W_TOP * G_SCALE), None, ALU.mult))
            then(v.tensor_scalar(bias[:], b_raw, c_(F_UP), None, ALU.mult))
            then(v.tensor_scalar(w_n, w_raw, c_(WSC), None, ALU.mult))
            w_n3 = w_n.rearrange("p (k i) -> p k i", k=KK)
            then(v.tensor_copy(dup_hi[:, :, 0, :], w_n3))
            then(v.tensor_copy(dup_hi[:, :, 1, :], dup_hi[:, :, 0, :]))
            then(v.tensor_tensor(dup_lo[:, :, 0, :], w_n3, dup_hi[:, :, 0, :], ALU.subtract))
            v.tensor_copy(dup_lo[:, :, 1, :], dup_lo[:, :, 0, :]).then_inc(dup_ready, 1)
            dve.wait_ge(rs_ready, 1)
            for g, be, mu, rs, s, t in ((GAM1, BET1, MU1, RS1, S1, T1), (GAM2, BET2, MU2, RS2, S2, T2)):
                then(v.tensor_tensor(c_(s), p_(g), c_(rs), ALU.mult))
                then(v.tensor_tensor(c_(TMP), c_(s), p_(mu), ALU.mult))
                then(v.tensor_tensor(c_(t), p_(be), c_(TMP), ALU.subtract))
            then(v.tensor_tensor(c_(SA), c_(S1), p_(A1), ALU.mult))
            then(v.tensor_scalar(c_(SG), c_(S1), 0.0, 2.0, ALU.is_ge, ALU.mult))
            then(v.tensor_scalar(c_(SG), c_(SG), -1.0, None, ALU.add))
            then(v.tensor_scalar(c_(NTAU), c_(SA), 0.0, -2.0, ALU.is_ge, ALU.mult))
            then(v.tensor_scalar(c_(NTAU), c_(NTAU), 1.0, None, ALU.add))
            then(v.tensor_tensor(c_(A_SC), c_(S1), c_(SG), ALU.mult))
            then(v.tensor_tensor(c_(A_BI), c_(T1), c_(SG), ALU.mult))
            then(v.tensor_tensor(c_(B_SC), c_(SA), c_(NTAU), ALU.mult))
            v.tensor_tensor(c_(B_BI), c_(T1), c_(NTAU), ALU.mult).then_inc(ab_bias_ready, 1)
            then(v.tensor_tensor(c_(C1), c_(S2), p_(A2), ALU.mult))
            then(v.tensor_tensor(c_(C2), c_(S2), c_(C1), ALU.subtract))
            dve.wait_ge(ident_ready, 1)
            v.tensor_copy(ident_bf[:], ident[:]).then_inc(signs_ready, 1)
            dve.wait_ge(act_set, 1)
            for k in range(KK):
                v.tensor_scalar(dw_diag[:, k, :], ident[:], dws[:, k:k + 1], None, ALU.mult)
            dve.wait_ge(w_turned, 1)
            for n, w in enumerate((w_hi, w_lo)):
                v.tensor_copy(w[:].rearrange("p k c -> p (k c)"), tap_ps[:, n, 0, :].bitcast(FP16)[:, 0:KK * C])
            dve.wait_ge(pw_turned, 1)
            v.tensor_copy(pw_k[:], dw_ps[:, 0:P]).then_inc(pwk_ready, 1)
            v.tensor_scalar(pw_a[:], dw_ps[:, 0:P], c_(SG), None, ALU.mult)
            v.tensor_scalar(pw_b[:], dw_ps[:, 0:P], c_(NTAU), None, ALU.mult)
            dve.wait_ge(k_ready, 1)
            then(v.tensor_scalar(c_(NEG_K), pw_ps[:, 0:1], -1.0, None, ALU.mult))
            then(v.tensor_tensor(c_(TMP), c_(NEG_K), c_(C1), ALU.mult))
            dve.wait_ge(act_set, 2)
            then(v.tensor_tensor(c_(Z_BI), c_(T2), c_(TMP), ALU.add))
            then(v.tensor_scalar(c_(SG2), c_(C2), 0.0, 2.0, ALU.is_ge, ALU.mult))
            then(v.tensor_scalar(c_(SG2), c_(SG2), -1.0, None, ALU.add))
            then(v.tensor_tensor(c_(C2_ABS), c_(C2), c_(SG2), ALU.mult))
            v.tensor_tensor(c_(NEG_KC), c_(NEG_K), c_(C2_ABS), ALU.mult)
            v.tensor_tensor(c_(C1_SG), c_(C1), c_(SG2), ALU.mult)
            v.tensor_scalar(c_(MEAN_SG), c_(SG2), -1.0 / N_GROUP, None, ALU.mult)
            v.tensor_tensor(c_(Z_BI_SG), c_(Z_BI), c_(SG2), ALU.mult).then_inc(consts_ready, 1)
            dve.wait_ge(consts_ready, 1)
            dve.wait_ge(pads_ready, 2)

            def s_(t, n):
                return st[:, t.slot, n:n + 1]

            PAIR = [i ^ 1 for i in range(32)]

            def pair_sum(t, src, tmp, shuf, dst, ready, done, extra):
                wait_apart(dve, ready, t.count(1, 1))
                v.stream_shuffle(tmp, src, PAIR).then_inc(shuf, 1)
                dve.wait_ge(shuf, t.count(1, 1))
                v.tensor_scalar(dst, src, tmp, extra, ALU.add, ALU.add).then_inc(done, 1)

            def mean0(t):
                pair_sum(t, s_(t, SUM0), s_(t, SH0), shuffled[0], s_(t, NM0), sum0_done, nm0_done, 0.0)

            def var0(t):
                pair_sum(t, s_(t, SQ0), s_(t, SHV0), shuffled[1], s_(t, VAR0), sq0_done, var0_done, EPS * N_GROUP)

            def mean1(t):
                pair_sum(t, s_(t, SUM1), SHM[:, t.slot, 0:1], shuffled[2], s_(t, NM1), sum1_done, nm1_done, 0.0)

            def var1(t):
                pair_sum(t, s_(t, SQ1), SHM[:, t.slot, 1:2], shuffled[3], SHM[:, t.slot, 2:3], sq1_done, var1_done, EPS * N_GROUP)

            def clamp(t, c):
                dve.wait_ge(ab_done, t.count(CHUNKS, c + 1))
                v.tensor_scalar(ab[:, c % 2, 0, :], ab[:, c % 2, 0, :], c_(CL_A), None, ALU.max)
                v.tensor_scalar(ab[:, c % 2, 1, :], ab[:, c % 2, 1, :], c_(CL_B), None, ALU.max).then_inc(clamped, 1)

            def x1_linear(t, c):
                if c == 0:
                    dve.wait_ge(z_done, t.count(1, 1))
                dve.wait_ge(relu_done, t.count(CHUNKS, c + 1))
                xc = xb[:, t.slot, c * CH:(c + 1) * CH]
                v.scalar_tensor_tensor(xc, pw_ps[:, 0:CH], c_(C1_SG), xc, ALU.mult, ALU.add).then_inc(y_done, 1)

            def centre_bias(t):
                wait_apart(dve, r1_done, t.count(1, 1))
                v.reciprocal(s_(t, B4), s_(t, QS)).then_inc(inverse_done, 1)
                wait_apart(dve, inverse_done, t.count(1, 1))
                v.tensor_tensor(s_(t, B4), s_(t, B4), bias[:, 4:5], ALU.add).then_inc(b4_done, 1)

            def low(t, half):
                dve.wait_ge(hi_done, t.count(2, half + 1))
                wait(dve, stacked[half], t.count(64))
                a, z = half * H // 2, (half + 1) * H // 2
                v.scalar_tensor_tensor(rows3(g_lo[:])[:, a:z, :], q[:, t.par, 1 + a:1 + z, 1:1 + WD], c_(G_UP),
                                       rows3(g_hi[:])[:, a:z, :], ALU.mult, ALU.subtract).then_inc(lo_done, 1)

            def product(t, u):
                qq, k = divmod(u, KK)
                n = PLACE[k]
                dy, dx = divmod(k, 3)
                if u == 0:
                    dve.wait_ge(q_done, t.count(1, 1))
                if u == 4:
                    dve.wait_ge(b4_done, t.count(1, 1))
                if k == 0:
                    wait(dve, folded, t.count(16 * 4, 16 * (qq - 1)))
                elif n in FREED:
                    wait(dve, added, t.count(4 * ADDS, ADDS * (qq - 2) + FREED[n]))
                dve.wait_ge(taps_ready, t.count(UNITS, u + 1))
                r = qq * QR + dy
                v.scalar_tensor_tensor(
                    prod[:, qq % 2, n, :].rearrange("p (j a b) -> p j a b", j=2, b=WD),
                    tap_ps[:, u % SLOTS, :, 0:CH].rearrange("p j (a b) -> p j a b", b=WD),
                    s_(t, B4) if k == 4 else bias[:, k:k + 1],
                    q[:, t.par, r:r + QR, dx:dx + WD].rearrange("p (j a) b -> p j a b", j=2),
                    ALU.add, ALU.mult).then_inc(prod_done, 1)

            def step(done, taps, mid, front, load):
                for u in range(UNITS):
                    for t, c in chunks_due(u, CLAMP_DELAY, mid, front):
                        clamp(t, c)
                    for t, c in chunks_due(u, X1_DELAY, mid, front):
                        x1_linear(t, c)
                    if taps:
                        product(taps, u)
                    for at, who, what in ((MEAN0_AT, front, mean0), (VAR0_AT, front, var0), (MEAN1_AT, mid, mean1),
                                          (VAR1_AT, mid, var1), (B4_AT, mid, centre_bias)):
                        if u == at and who:
                            what(who)
                    for half in range(2):
                        if mid and u == LOW_AT[half]:
                            low(mid, half)

            program(step, dve.Fori)


FIRST_CHUNK = 13
CHUNK_EVERY = 4
CLAMP_DELAY = 2
PW_DELAY = 5
X1_DELAY = 6
SUM0_AT = 0
MEAN0_AT = 2
SQUARE0_AT = 3
VAR0_AT = 5
R0_AT = 6
SIGN0_AT = 7
AFFINE0_AT = 9
SUM1_AT = 13
MEAN1_AT = 15
SQUARE1_AT = 16
VAR1_AT = 18
R1_AT = 19
Q_AT = 20
HI_AT = (21, 22)
B4_AT = 23
LOW_AT = (25, 27)
MEAN_DELAY = 1
ADD_DELAY = 6
OUT_DELAY = 11
PLACE = (4, 5, 6, 7, 3, 1, 2, 0, 8)
FREED = {3: 1, 1: 2, 2: 3, 0: 4, 8: 4}

_INS = ["x", "L0_conv_dw_weight", "L0_conv_prelu1_a", "L0_conv_bn1_gamma", "L0_conv_bn1_beta", "L0_conv_bn1_mean",
        "L0_conv_bn1_var", "L0_conv_pw_weight", "L0_conv_prelu2_a", "L0_conv_bn2_gamma", "L0_conv_bn2_beta",
        "L0_conv_bn2_mean", "L0_conv_bn2_var", "L1_conv_W", "L1_conv_b"]


def kernel(**inputs):
    import numpy as _np
    import concourse.bacc as _bacc
    from concourse import mybir as _mybir
    from concourse.bass_utils import run_bass_kernel_spmd as _run

    nc = _bacc.Bacc("TRN2", target_bir_lowering=False, num_devices=1)
    arrays, args = {}, []
    for name in _INS:
        a = _np.ascontiguousarray(inputs[name])
        arrays[f"in_{name}_dram"] = a
        args.append(nc.dram_tensor(f"in_{name}_dram", a.shape, _mybir.dt.from_np(a.dtype), kind="ExternalInput").ap())
    shape = inputs["x"].shape
    args.append(nc.dram_tensor("out_0_dram", shape, _mybir.dt.from_np(_np.dtype("float32")), kind="ExternalOutput").ap())
    preact_involution_kernel(nc, *args)
    r = _run(nc, [arrays], core_ids=[0])
    return r.results[0]["out_0_dram"]
```

```python
from contextlib import ExitStack

import concourse.bass as bass
from concourse import mybir

F32 = mybir.dt.float32
BF16 = mybir.dt.bfloat16
FP16 = mybir.dt.float16
U32 = mybir.dt.uint32
ALU = mybir.AluOpType
ACT = mybir.ActivationFunctionType
AX = mybir.AxisListType

P = 128
RING = 4
EPS = 1e-5
G_SCALE = 2.0 ** 9
W_TOP = 2.0 ** 14
W_FLOOR = 2.0 ** -40


def preact_involution_kernel(nc, x, dw, a1, gam1, bet1, mu1, var1, pw, a2, gam2, bet2, mu2, var2, W, b, out):
    B, C, H, WD = x.shape
    KK = 9
    NPIX = H * WD
    TILES = B * C // P
    ROWS = 7
    CH = ROWS * WD
    CHUNKS = H // ROWS
    QUARTERS = CHUNKS // 2
    QP = 2 * CH
    QR = 2 * ROWS
    HP, WP = H + 2, WD + 2
    UNITS = QUARTERS * KK
    SLOTS = 3
    ADDS = 4
    N_GROUP = 2 * NPIX
    assert P == 2 * C and TILES % RING == 0 and UNITS % SLOTS == 0 and CH <= 512

    x_t = x.rearrange("(n s) c h w -> n (s c) (h w)", s=2)
    out_t = out.rearrange("(n s) c h w -> n (s c) (h w)", s=2)

    with ExitStack() as ctx:
        def sb(name, shape, dt):
            return ctx.enter_context(nc.sbuf_tensor(name, shape, dt))

        def sem(name):
            return ctx.enter_context(nc.semaphore(name))

        xb = sb("xb", [P, RING, NPIX], F32)
        signs = sb("signs", [P, HP, WP], BF16)
        q = sb("q", [P, 2, HP, WP], F32)
        g_hi = sb("g_hi", [P, NPIX], FP16)
        g_lo = sb("g_lo", [P, NPIX], FP16)
        stack = sb("stack", [P, 2, 2, NPIX], FP16)
        unused = sb("unused", [P, NPIX], BF16)
        ab = sb("ab", [P, 2, 2, CH], BF16)
        relu = sb("relu", [P, 2, CH], F32)
        prod = sb("prod", [P, 2, KK, QP], F32)
        ob = sb("ob", [P, 2, QP], F32)
        st = sb("st", [P, RING, 23], F32)
        ident = sb("ident", [P, P], FP16)
        ident_bf = sb("ident_bf", [P, P], BF16)
        pw_k = sb("pw_k", [P, P], BF16)
        dw_diag = sb("dw_diag", [P, KK, P], BF16)
        pw_block = sb("pw_block", [P, P], BF16)
        pw_a = sb("pw_a", [P, P], BF16)
        pw_b = sb("pw_b", [P, P], BF16)
        w_hi = sb("w_hi", [P, KK, C], FP16)
        w_lo = sb("w_lo", [P, KK, C], FP16)
        bias = sb("bias", [P, KK], F32)
        col = sb("col", [P, 43], F32)
        minus_half = sb("minus_half", [P, 2], F32)
        minus_k_terms = sb("minus_k_terms", [P, 1], BF16)
        dws = sb("dws", [P, KK], F32)
        RAW = KK * C + C + 2 * KK + 10
        raw = prod[:, 0, 0, 0:RAW]
        LARGE = KK * C + KK
        w_raw, b_raw = raw[:, 0:KK * C], raw[:, KK * C:LARGE]
        pw_raw, dw_raw = raw[:, LARGE:LARGE + C], raw[:, LARGE + C:LARGE + C + KK]
        prm = raw[:, RAW - 10:RAW]
        w_n = prod[:, 0, 1, 0:KK * C]
        dup_hi = prod[:, 0, 2, :].bitcast(FP16)[:, 0:KK * P].rearrange("p (k d i) -> p k d i", k=KK, d=2)
        dup_lo = prod[:, 0, 4, :].bitcast(FP16)[:, 0:KK * P].rearrange("p (k d i) -> p k d i", k=KK, d=2)

        tap_ps = ctx.enter_context(nc.psum_tensor("tap_ps", [P, SLOTS, 2, 512], F32))
        dw_ps = ctx.enter_context(nc.psum_tensor("dw_ps", [P, 512], F32))
        pw_ps = ctx.enter_context(nc.psum_tensor("pw_ps", [P, 512], F32))

        A1, GAM1, BET1, MU1, VAR1, A2, GAM2, BET2, MU2, VAR2 = range(10)
        (RS1, RS2,
         S1, SA, T1, S2, T2,
         SG, NTAU, A_SC, B_SC, A_BI, B_BI,
         HALF_T0, NEG_HALF_T0, KEEP_A, KEEP_B, STEP_A, STEP_B, W_A, W_B,
         C1, C2, NEG_K, Z_BI,
         WMAX, WPOW, WINV, WSC,
         F_UP, G_UP, G_DOWN,
         TMP, VE1, VE2,
         SG2, C2_ABS, C1_SG, NEG_KC, Z_BI_SG,
         MEAN_SG, ROOT_SG, ROOT_DOWN) = range(43)
        SUM0, SH0, NM0, SQ0, SHV0, VAR0, RP0, R0, ZS, ZB = range(10)
        SUM1, SH1, NM1, SQ1, SHV1, VARIANCE1, RP1, QS, QB, B4, INV1, QS_SG, MEAN1 = range(10, 23)
        sums = sb("sums", [P, 2, 2, CHUNKS], F32)
        scaled = sb("scaled", [P, 2 * CHUNKS], F32)

        def c_(n):
            return col[:, n:n + 1]

        def two(n):
            return col[:, n:n + 2]

        def p_(n):
            return prm[:, n:n + 1]

        params_in, bn2_in, weights_in = sem("params_in"), sem("bn2_in"), sem("weights_in")
        w_in, w_both_in = sem("w_in"), sem("w_both_in")
        ident_ready, pads_ready, half_ready = sem("ident_ready"), sem("pads_ready"), sem("half_ready")
        pool_set, dve_set, act_set = sem("pool_set"), sem("dve_set"), sem("act_set")
        var_eps_ready, rs_ready, signs_ready = sem("var_eps_ready"), sem("rs_ready"), sem("signs_ready")
        dup_ready, w_turned, pw_turned, k_ready, pwk_ready = sem("dup_ready"), sem("w_turned"), sem("pw_turned"), sem("k_ready"), sem("pwk_ready")
        consts_ready, w_copied = sem("consts_ready"), sem("w_copied")
        x_loaded = [sem(f"x_loaded{i}") for i in range(RING)]
        sum0_done, nm0_done, sq0_done, var0_done, r0_done = sem("sum0_done"), sem("nm0_done"), sem("sq0_done"), sem("var0_done"), sem("r0_done")
        signs_done, z_done = sem("signs_done"), sem("z_done")
        sum1_done, nm1_done, sq1_done, var1_done, r1_done = sem("sum1_done"), sem("nm1_done"), sem("sq1_done"), sem("var1_done"), sem("r1_done")
        shuffled = [sem(f"shuffled_{name}") for name in ("mean0", "var0", "mean1", "var1")]
        pow0_done, pow1_done, r0_step, r1_step = sem("pow0_done"), sem("pow1_done"), sem("r0_step"), sem("r1_step")
        last_summed = sem("last_summed")
        q_done, inverse_done, b4_done = sem("q_done"), sem("inverse_done"), sem("b4_done")
        hi_done, lo_done = sem("hi_done"), sem("lo_done")
        stacked = [sem("stacked0"), sem("stacked1")]
        dw_ready, ab_done, pw_ready, relu_done, y_done, x1_done = (
            sem("dw_ready"), sem("ab_done"), sem("pw_ready"), sem("relu_done"), sem("y_done"), sem("x1_done"))
        taps_ready, prod_done, added = sem("taps_ready"), sem("prod_done"), sem("added")
        folded, mean_added = sem("folded"), sem("mean_added")
        stored = [sem("stored0"), sem("stored1")]

        def wait(eng, s, value):
            if isinstance(value, int) and value <= 0:
                return
            eng.wait_ge(s, value)

        def wait_apart(eng, s, value):
            if not isinstance(value, int):
                value = eng.to_reg(value)
                eng.wait_ge(consts_ready, 1)
            wait(eng, s, value)

        class Tile:

            def __init__(self, h, off):
                self.h, self.off = h, off
                self.slot, self.par = off % RING, off % 2
                self.first = isinstance(h, int) and RING * h + off == 0
                self.last = isinstance(h, int) and RING * h + off == TILES - 1

            def count(self, per, plus=0):
                assert isinstance(self.h, int) or self.off * per + plus > 0
                return self.h * (RING * per) + (self.off * per + plus)

            def rounds(self, per=16):
                return self.h * per + (self.off // RING + 1) * per

            def index(self):
                return self.h * RING + self.off

        def program(step, loop):
            def peeled(i):
                step(*(Tile(0, i + d) if 0 <= i + d < TILES else None for d in range(-1, 4)))

            for i in range(-3, 1):
                peeled(i)
            with loop(0, (TILES - 4) // RING) as h:
                for off in range(1, 1 + RING):
                    step(*(Tile(h, off + d) for d in range(-1, 4)))
            for i in range(TILES - 3, TILES + 1):
                peeled(i)

        def due(u, delay, first, every, count, now, later):
            for piece in range(count):
                at = first + every * piece + delay
                tile = now if at < UNITS else later
                if tile and at % UNITS == u:
                    yield tile, piece

        def chunks_due(u, delay, mid, front):
            return due(u, delay, FIRST_CHUNK, CHUNK_EVERY, CHUNKS, front, mid)

        def quarters_due(u, delay, done, taps):
            return due(u, delay, KK, KK, QUARTERS, taps, done)

        def rows3(ap):
            return ap.rearrange("p (a b) -> p a b", b=WD)

        block = ctx.enter_context(nc.Block())

        @block.sync
        def _(sp):
            for n, v in enumerate((a1, gam1, bet1, mu1, var1)):
                sp.dma_start(prm[0:C, n:n + 1], v.rearrange("(c a) -> c a", a=1)).then_inc(params_in, 16)
            sp.dma_start(pw_raw[0:C, :], pw).then_inc(params_in, 16)
            sp.dma_start(dw_raw[0:C, :], dw.rearrange("c a i j -> c (a i j)")).then_inc(params_in, 16)
            sp.dma_start(xb[:, 0, :], x_t[0:1].rearrange("a p n -> (a p) n")).then_inc(x_loaded[0], 16)
            sp.dma_start(w_raw[0:C, :].rearrange("c (k i) -> c k i", k=KK), W.rearrange("(c k) i -> c k i", k=KK)).then_inc(w_in, 16)
            sp.dma_start(b_raw[0:C, :], b.rearrange("(c k) -> c k", k=KK)).then_inc(w_in, 16)
            sp.wait_ge(params_in, 16 * 7)
            sp.wait_ge(bn2_in, 16 * 5)
            sp.dma_start(raw[C:P, LARGE:RAW], raw[0:C, LARGE:RAW]).then_inc(weights_in, 16)
            sp.wait_ge(w_in, 16 * 2)
            sp.dma_start(raw[C:P, 0:LARGE], raw[0:C, 0:LARGE]).then_inc(w_both_in, 16)

            def store(t, qq):
                if t.last and qq == QUARTERS - 1:
                    sp.wait_ge(last_summed, 4)
                else:
                    wait_apart(sp, added, t.count(4 * ADDS, ADDS * (qq + 1)))
                sp.dma_start(out_t[bass.ds(t.index(), 1), :, qq * QP:(qq + 1) * QP].rearrange("a p n -> (a p) n"),
                             ob[:, qq % 2, :]).then_inc(stored[qq % 2], 16)

            def stack_half(t, half):
                wait_apart(sp, lo_done, t.count(2, half + 1))
                a, z = half * NPIX // 2, (half + 1) * NPIX // 2
                for s in range(2):
                    own = slice(s * C, s * C + C)
                    for dst, src in ((slice(0, C), g_hi), (slice(C, P), g_lo)):
                        sp.dma_start(stack[dst, t.par, s, a:z], src[own, a:z]).then_inc(stacked[half], 16)

            def step(done, taps, mid, front, load):
                if load and not load.first:
                    wait_apart(sp, q_done, load.count(1, -3))
                    sp.dma_start(xb[:, load.slot, :],
                                 x_t[bass.ds(load.index(), 1)].rearrange("a p n -> (a p) n")).then_inc(x_loaded[load.slot], 16)
                for u in range(UNITS):
                    for t, qq in quarters_due(u, OUT_DELAY + 1, done, taps):
                        store(t, qq)
                    for half in range(2):
                        if mid and u == LOW_AT[half] + 1:
                            if half == 0:
                                wait_apart(sp, taps_ready, mid.count(UNITS, -UNITS))
                            stack_half(mid, half)

            program(step, sp.Fori)
            for s in stored:
                sp.wait_ge(s, 16 * 2 * TILES)

        @block.gpsimd
        def _(pool):
            pool.memset(minus_half[:], -0.5).then_inc(pool_set, 1)
            pool.memset(ident[:], 0.0).then_inc(pool_set, 1)
            for n, v in enumerate((a2, gam2, bet2, mu2, var2)):
                pool.dma_start(prm[0:C, 5 + n:6 + n], v.rearrange("(c a) -> c a", a=1)).then_inc(bn2_in, 16)
            pool.memset(pw_block[:], 0.0).then_inc(half_ready, 1)
            pool.wait_ge(pool_set, 2)
            pool.affine_select(out=ident[:], in_=ident[:], compare_op=ALU.not_equal, fill=1.0, base=0,
                               pattern=[[-1, P]], channel_multiplier=1).then_inc(ident_ready, 1)
            pool.wait_ge(var_eps_ready, 1)
            pool.tensor_tensor(col[:, RS1:RS2 + 1], col[:, VE1:VE2 + 1], minus_half[:], ALU.pow).then_inc(rs_ready, 1)
            pool.wait_ge(consts_ready, 1)

            def s_(t, n):
                return st[:, t.slot, n:n + 1]

            def rstd(t, shuf, own, other, var, var_done, power, pow_done):
                wait_apart(pool, shuf, t.count(1, 1))
                pool.tensor_scalar(s_(t, var), s_(t, own), s_(t, other), EPS * N_GROUP, ALU.add, ALU.add).then_inc(var_done, 1)
                wait_apart(pool, var_done, t.count(1, 1))
                pool.tensor_tensor(s_(t, power), s_(t, var), minus_half[:, 0:1], ALU.pow).then_inc(pow_done, 1)

            def rstd0(t):
                rstd(t, shuffled[1], SQ0, SHV0, VAR0, var0_done, RP0, pow0_done)

            def rstd1(t):
                rstd(t, shuffled[3], SQ1, SHV1, VARIANCE1, var1_done, RP1, pow1_done)

            def add(dst, a, c):
                return pool.tensor_tensor(dst, a, c, ALU.add).then_inc(added, 1)

            def products(qq):
                return [prod[:, qq % 2, n, :] for n in range(KK)]

            def fold(t, qq):
                wait_apart(pool, prod_done, t.count(UNITS, KK * qq + KK - 1))
                pool.dma_start(prod[:, qq % 2, 0:4, :], prod[:, qq % 2, 4:8, :], accum_op=ALU.add,
                               max_dma_last_dim=4 * QP).then_inc(folded, 16)

            def add23(t, qq):
                pr = products(qq)
                pool.wait_ge(folded, t.count(16 * 4, 16 * (qq + 1)))
                add(pr[2], pr[2], pr[3])

            def add01(t, qq):
                pr = products(qq)
                add(pr[0], pr[0], pr[1])

            def add02(t, qq):
                pr = products(qq)
                pool.wait_ge(added, t.count(4 * ADDS, ADDS * qq + 2))
                add(pr[0], pr[0], pr[2])

            def final(t, qq):
                pr = products(qq)
                wait_apart(pool, mean_added, t.count(4, qq + 1))
                wait_apart(pool, stored[qq % 2], t.count(16 * 2, 16 * (qq // 2)))
                wait_apart(pool, added, t.count(4 * ADDS, ADDS * qq + 3))
                add(ob[:, qq % 2, :], pr[8], pr[0])

            def x1_relu(t, c):
                wait_apart(pool, relu_done, t.count(CHUNKS, c + 1))
                wait_apart(pool, y_done, t.count(CHUNKS, c + 1))
                xc = xb[:, t.slot, c * CH:(c + 1) * CH]
                pool.tensor_tensor(xc, xc, relu[:, c % 2, :], ALU.add).then_inc(x1_done, 1)

            def step(done, taps, mid, front, load):
                for u in range(UNITS):
                    for what, delay in ((fold, 0), (add23, ADD23_DELAY), (add01, ADD01_DELAY), (add02, ADD02_DELAY),
                                        (final, OUT_DELAY)):
                        for t, qq in quarters_due(u, delay, done, taps):
                            if not (t.last and qq == QUARTERS - 1):
                                what(t, qq)
                    for t, c in chunks_due(u, RELU_DELAY, mid, front):
                        x1_relu(t, c)
                    if front and u == R0_AT:
                        rstd0(front)
                    if mid and u == R1_AT:
                        rstd1(mid)

            program(step, pool.Fori)

        @block.tensor
        def _(pe):
            pe.wait_ge(ident_ready, 1)
            pe.wait_ge(signs_ready, 2)
            pe.matmul(dw_ps[:, 0:P], pw_block[:], ident_bf[:], start=True, stop=True).then_inc(pw_turned, 1)
            pe.wait_ge(pwk_ready, 1)
            pe.matmul(pw_ps[:, 0:1], pw_k[:], minus_k_terms[:], start=True, stop=True).then_inc(k_ready, 1)
            pe.wait_ge(consts_ready, 1)

            def turn_w():
                pe.wait_ge(dup_ready, 1)
                wt = [tap_ps[:, n, 0, :].bitcast(FP16)[:, 0:KK * C].rearrange("p (k c) -> p k c", k=KK) for n in range(2)]
                for n, d in enumerate((dup_hi, dup_lo)):
                    for k in range(KK):
                        last = pe.transpose(wt[n][:, k, :], d[0:C, k, :, :].rearrange("p d i -> p (d i)"), ident[0:C, 0:C])
                last.then_inc(w_turned, 1)

            def unit(t, u):
                qq, k = divmod(u, KK)
                wait(pe, prod_done, t.count(UNITS, u + 1 - SLOTS))
                for half in range(2):
                    if u == half * UNITS // 2:
                        pe.wait_ge(stacked[half], t.count(64, 64))
                for j in range(2):
                    a = (2 * qq + j) * CH
                    for w in (w_hi, w_lo):
                        for s in range(2):
                            mm = pe.matmul(tap_ps[s * C:s * C + C, u % SLOTS, j, 0:CH], w[:, k, :],
                                           stack[:, t.par, s, a:a + CH], start=(w is w_hi), stop=(w is w_lo))
                mm.then_inc(taps_ready, 1)

            def depthwise(t, c, taps):
                if c == 0 and taps.start == 0:
                    pe.wait_ge(signs_done, t.count(1, 1))
                if taps.start == 0:
                    wait(pe, ab_done, t.count(CHUNKS, c))
                for k in taps:
                    dy, dx = divmod(k, 3)
                    mm = pe.matmul(rows3(dw_ps[:, 0:CH]), dw_diag[:, k, :],
                                   signs[:, c * ROWS + dy:c * ROWS + dy + ROWS, dx:dx + WD],
                                   start=(k == 0), stop=(k == KK - 1))
                if taps.stop == KK:
                    mm.then_inc(dw_ready, 1)

            def pointwise(t, c):
                pe.wait_ge(ab_done, t.count(CHUNKS, c + 1))
                wait(pe, y_done, t.count(CHUNKS, c))
                pe.matmul(pw_ps[:, 0:CH], pw_a[:], ab[:, c % 2, 0, :], start=True, stop=False)
                pe.matmul(pw_ps[:, 0:CH], pw_b[:], ab[:, c % 2, 1, :], start=False, stop=True).then_inc(pw_ready, 1)

            def step(done, taps, mid, front, load):
                for u in range(UNITS):
                    if mid and mid.first and u == TURN_AT:
                        turn_w()
                    if taps and taps.first and u == 0:
                        pe.wait_ge(w_copied, 1)
                    if taps:
                        unit(taps, u)
                    for t, c in chunks_due(u, 0, mid, front):
                        depthwise(t, c, range(0, 5))
                    for t, c in chunks_due(u, 1, mid, front):
                        depthwise(t, c, range(5, KK))
                    for t, c in chunks_due(u, PW_DELAY, mid, front):
                        pointwise(t, c)

            program(step, pe.Fori)

        @block.scalar
        def _(act):
            def acts(o, i, f, **kw):
                return nc.scalar.activation(o, i, f, **kw)

            act.wait_ge(weights_in, 16)
            act.wait_ge(half_ready, 1)
            acts(dws[:], dw_raw, ACT.Sign).then_inc(act_set, 1)
            acts(pw_block[0:C, 0:C], pw_raw[0:C, :], ACT.Sign)
            acts(pw_block[C:P, C:P], pw_raw[C:P, :], ACT.Sign).then_inc(signs_ready, 1)

            def s_(t, n):
                return st[:, t.slot, n:n + 1]

            def conv_act(t, c):
                act.wait_ge(dw_ready, t.count(CHUNKS, c + 1))
                wait(act, pw_ready, t.count(CHUNKS, c - 1))
                acts(ab[:, c % 2, 0, :], dw_ps[:, 0:CH], ACT.Sign, scale=c_(A_SC), bias=c_(A_BI))
                acts(ab[:, c % 2, 1, :], dw_ps[:, 0:CH], ACT.Sign, scale=c_(B_SC), bias=c_(B_BI)).then_inc(ab_done, 1)

            def relu_act(t, c):
                act.wait_ge(pw_ready, t.count(CHUNKS, c + 1))
                wait(act, x1_done, t.count(CHUNKS, c - 1))
                acts(relu[:, c % 2, :], pw_ps[:, 0:CH], ACT.Relu, scale=c_(C2_ABS), bias=c_(NEG_KC),
                     accum_out=sums[:, t.par, 1, c:c + 1]).then_inc(relu_done, 1)

            def sum0(t):
                act.wait_ge(x_loaded[t.slot], t.rounds())
                wait(act, sq1_done, t.count(1, -1))
                acts(unused[:], xb[:, t.slot, :], ACT.Copy, scale=-1.0 / N_GROUP, accum_out=s_(t, SUM0)).then_inc(sum0_done, 1)

            def square0(t):
                act.wait_ge(shuffled[0], t.count(1, 1))
                acts(s_(t, NM0), s_(t, SUM0), ACT.Identity, bias=s_(t, SH0)).then_inc(nm0_done, 1)
                act.wait_ge(nm0_done, t.count(1, 1))
                acts(unused[:], xb[:, t.slot, :], ACT.Square, bias=s_(t, NM0), accum_out=s_(t, SQ0)).then_inc(sq0_done, 1)

            def sum1(t):
                act.wait_ge(y_done, t.count(CHUNKS, CHUNKS))
                act.wait_ge(relu_done, t.count(CHUNKS, CHUNKS))
                wait(act, sum1_done, t.count(1, 0))
                acts(scaled[:], sums[:, t.par, :, :].rearrange("p a b -> p (a b)"), ACT.Copy, scale=c_(MEAN_SG),
                     accum_out=s_(t, SUM1)).then_inc(sum1_done, 1)

            def square1(t, front):
                act.wait_ge(x1_done, t.count(CHUNKS, CHUNKS))
                act.wait_ge(shuffled[2], t.count(1, 1))
                acts(s_(t, NM1), s_(t, SUM1), ACT.Identity, bias=s_(t, SH1)).then_inc(nm1_done, 1)
                act.wait_ge(nm1_done, t.count(1, 1))
                if front:
                    act.wait_ge(sq0_done, front.count(1, 1))
                else:
                    wait(act, sq1_done, t.count(1, 0))
                acts(unused[:], xb[:, t.slot, :], ACT.Square, scale=c_(SG2), bias=s_(t, NM1), accum_out=s_(t, SQ1)).then_inc(sq1_done, 1)

            def sign0(t):
                wait(act, dw_ready, t.count(CHUNKS))
                acts(signs[:, 1:1 + H, 1:1 + WD], rows3(xb[:, t.slot, :]), ACT.Sign, bias=s_(t, NM0)).then_inc(signs_done, 1)

            def affine0(t):
                act.wait_ge(pow0_done, t.count(1, 1))
                acts(s_(t, R0), s_(t, RP0), ACT.Copy, scale=c_(ROOT_SG)).then_inc(r0_step, 1)
                act.wait_ge(r0_step, t.count(1, 1))
                acts(s_(t, ZS), s_(t, R0), ACT.Identity, bias=c_(SG2))
                acts(s_(t, ZB), s_(t, NM0), ACT.Identity, scale=s_(t, R0), bias=c_(Z_BI_SG)).then_inc(r0_done, 1)
                act.wait_ge(r0_done, t.count(1, 1))
                acts(xb[:, t.slot, :], xb[:, t.slot, :], ACT.Identity, scale=s_(t, ZS), bias=s_(t, ZB)).then_inc(z_done, 1)

            def q_pass(t):
                if t.first:
                    act.wait_ge(dup_ready, 1)
                act.wait_ge(pow1_done, t.count(1, 1))
                acts(s_(t, QS), s_(t, RP1), ACT.Copy, scale=c_(ROOT_DOWN)).then_inc(r1_step, 1)
                acts(s_(t, MEAN1), s_(t, NM1), ACT.Copy, scale=-1.0)
                act.wait_ge(r1_step, t.count(1, 1))
                acts(s_(t, QS_SG), s_(t, QS), ACT.Copy, scale=c_(SG2))
                acts(s_(t, QB), s_(t, NM1), ACT.Copy, scale=s_(t, QS)).then_inc(r1_done, 1)
                act.wait_ge(r1_done, t.count(1, 1))
                wait(act, prod_done, t.count(UNITS, -UNITS))
                acts(q[:, t.par, 1:1 + H, 1:1 + WD], rows3(xb[:, t.slot, :]), ACT.Identity,
                     scale=s_(t, QS_SG), bias=s_(t, QB)).then_inc(q_done, 1)

            def hi_half(t, half):
                act.wait_ge(q_done, t.count(1, 1))
                wait(act, stacked[half], t.count(64))
                a, z = half * H // 2, (half + 1) * H // 2
                acts(rows3(g_hi[:])[:, a:z, :], q[:, t.par, 1 + a:1 + z, 1:1 + WD], ACT.Copy,
                     scale=c_(G_UP)).then_inc(hi_done, 1)

            def centre_bias(t):
                act.wait_ge(inverse_done, t.count(1, 1))
                acts(s_(t, B4), s_(t, INV1), ACT.Identity, bias=bias[:, 4:5]).then_inc(b4_done, 1)

            def add_mean(t, qq):
                act.wait_ge(prod_done, t.count(UNITS, KK * qq + KK))
                acts(prod[:, qq % 2, 8, :], prod[:, qq % 2, 8, :], ACT.Identity, bias=s_(t, MEAN1)).then_inc(mean_added, 1)

            sum0(Tile(0, 0))
            square0(Tile(0, 0))
            act.wait_ge(pads_ready, 2)
            sign0(Tile(0, 0))
            act.wait_ge(consts_ready, 1)

            def step(done, taps, mid, front, load):
                for u in range(UNITS):
                    for t, qq in quarters_due(u, MEAN_DELAY, done, taps):
                        add_mean(t, qq)
                    for t, c in chunks_due(u, AB_DELAY, mid, front):
                        conv_act(t, c)
                    for t, c in chunks_due(u, PW_DELAY, mid, front):
                        relu_act(t, c)
                    if front:
                        for at, what in ((SUM0_AT, sum0), (SQUARE0_AT, square0), (SIGN0_AT, sign0), (AFFINE0_AT, affine0)):
                            if u == at and not (front.first and what is not affine0):
                                what(front)
                    if mid and u == SUM1_AT:
                        sum1(mid)
                    if mid and u == B4_AT + 1:
                        centre_bias(mid)
                    if mid and u == SQUARE1_AT:
                        square1(mid, front)
                    if mid and u == Q_AT:
                        q_pass(mid)
                    for half in range(2):
                        if mid and u == HI_AT[half]:
                            hi_half(mid, half)

            program(step, act.Fori)

        @block.vector
        def _(dve):
            v = nc.vector
            steps = [0]

            def then(ins):
                steps[0] += 1
                ins.then_inc(dve_set, 1)
                dve.wait_ge(dve_set, steps[0])

            def s_(t, n):
                return st[:, t.slot, n:n + 1]

            PAIR = [i ^ 1 for i in range(32)]

            def shuffle(t, ready, own, other, shuf):
                wait_apart(dve, ready, t.count(1, 1))
                v.stream_shuffle(s_(t, other), s_(t, own), PAIR).then_inc(shuf, 1)

            def mean0(t):
                shuffle(t, sum0_done, SUM0, SH0, shuffled[0])

            def var0(t):
                shuffle(t, sq0_done, SQ0, SHV0, shuffled[1])

            def mean1(t):
                shuffle(t, sum1_done, SUM1, SH1, shuffled[2])

            def var1(t):
                shuffle(t, sq1_done, SQ1, SHV1, shuffled[3])

            v.memset(signs[:], 0.0).then_inc(pads_ready, 1)
            v.memset(q[:], 0.0).then_inc(pads_ready, 1)
            dve.wait_ge(weights_in, 16)
            v.tensor_scalar(c_(VE1), p_(VAR1), EPS, None, ALU.add)
            v.tensor_scalar(c_(VE2), p_(VAR2), EPS, None, ALU.add).then_inc(var_eps_ready, 1)
            dve.wait_ge(ident_ready, 1)
            v.tensor_copy(ident_bf[:], ident[:]).then_inc(signs_ready, 1)
            dve.wait_ge(act_set, 1)
            for k in range(KK):
                v.tensor_scalar(dw_diag[:, k, :], ident[:], dws[:, k:k + 1], None, ALU.mult)
            dve.wait_ge(rs_ready, 1)
            for g, be, mu, rs, s, t in ((GAM1, BET1, MU1, RS1, S1, T1), (GAM2, BET2, MU2, RS2, S2, T2)):
                then(v.tensor_tensor(c_(s), p_(g), c_(rs), ALU.mult))
                then(v.tensor_tensor(c_(TMP), c_(s), p_(mu), ALU.mult))
                then(v.tensor_tensor(c_(t), p_(be), c_(TMP), ALU.subtract))
            then(v.tensor_tensor(c_(SA), c_(S1), p_(A1), ALU.mult))
            mean0(Tile(0, 0))
            then(v.tensor_scalar(c_(SG), c_(S1), 0.0, 2.0, ALU.is_ge, ALU.mult))
            then(v.tensor_scalar(c_(SG), c_(SG), -1.0, None, ALU.add))
            then(v.tensor_scalar(c_(NTAU), c_(SA), 0.0, -2.0, ALU.is_ge, ALU.mult))
            then(v.tensor_scalar(c_(NTAU), c_(NTAU), 1.0, None, ALU.add))
            then(v.tensor_tensor(two(A_SC), two(S1), two(SG), ALU.mult))
            then(v.tensor_scalar(two(A_BI), two(SG), c_(T1), None, ALU.mult))
            then(v.tensor_scalar(c_(HALF_T0), c_(T1), 0.0, 0.5, ALU.is_equal, ALU.mult))
            v.tensor_scalar(c_(NEG_HALF_T0), c_(HALF_T0), -1.0, None, ALU.mult)
            v.tensor_scalar(two(KEEP_A), two(A_BI), 0.0, None, ALU.is_le)
            v.tensor_scalar(c_(TMP), c_(HALF_T0), -1.0, 1.0, ALU.mult, ALU.add)
            then(v.tensor_scalar(two(STEP_A), two(A_SC), 0.0, c_(HALF_T0), ALU.not_equal, ALU.mult))
            v.tensor_scalar(two(W_A), two(SG), c_(TMP), None, ALU.mult)
            v.scalar_tensor_tensor(c_(A_BI), c_(A_SC), c_(NEG_HALF_T0), c_(A_BI), ALU.mult, ALU.add)
            then(v.scalar_tensor_tensor(c_(B_BI), c_(B_SC), c_(HALF_T0), c_(B_BI), ALU.mult, ALU.add))
            v.tensor_tensor(two(A_SC), two(A_SC), two(KEEP_A), ALU.mult)
            v.tensor_tensor(two(STEP_A), two(STEP_A), two(SG), ALU.mult)
            then(v.tensor_scalar(c_(NEG_K), c_(T1), 0.0, None, ALU.is_gt))
            then(v.scalar_tensor_tensor(c_(NEG_K), c_(T1), 0.0, c_(NEG_K), ALU.is_lt, ALU.subtract))
            then(v.tensor_tensor(c_(NEG_K), c_(NEG_K), c_(STEP_A), ALU.add))
            then(v.tensor_tensor(minus_k_terms[:], c_(NEG_K), c_(STEP_B), ALU.add))
            then(v.tensor_tensor(c_(C1), c_(S2), p_(A2), ALU.mult))
            then(v.tensor_tensor(c_(C2), c_(S2), c_(C1), ALU.subtract))
            dve.wait_ge(pw_turned, 1)
            v.tensor_copy(pw_k[:], dw_ps[:, 0:P]).then_inc(pwk_ready, 1)
            v.tensor_scalar(pw_a[:], dw_ps[:, 0:P], c_(W_A), None, ALU.mult)
            v.tensor_scalar(pw_b[:], dw_ps[:, 0:P], c_(W_B), None, ALU.mult)
            dve.wait_ge(k_ready, 1)
            then(v.tensor_copy(c_(NEG_K), pw_ps[:, 0:1]))
            then(v.tensor_tensor(c_(TMP), c_(NEG_K), c_(C1), ALU.mult))
            then(v.tensor_tensor(c_(Z_BI), c_(T2), c_(TMP), ALU.add))
            then(v.tensor_scalar(c_(SG2), c_(C2), 0.0, 2.0, ALU.is_ge, ALU.mult))
            then(v.tensor_scalar(c_(SG2), c_(SG2), -1.0, None, ALU.add))
            then(v.tensor_tensor(c_(C2_ABS), c_(C2), c_(SG2), ALU.mult))
            v.tensor_tensor(c_(NEG_KC), c_(NEG_K), c_(C2_ABS), ALU.mult)
            v.tensor_tensor(c_(C1_SG), c_(C1), c_(SG2), ALU.mult)
            v.tensor_scalar(c_(ROOT_SG), c_(SG2), float(N_GROUP) ** 0.5, None, ALU.mult)
            v.tensor_scalar(c_(MEAN_SG), c_(SG2), -1.0 / N_GROUP, None, ALU.mult)
            v.tensor_tensor(c_(Z_BI_SG), c_(Z_BI), c_(SG2), ALU.mult).then_inc(consts_ready, 1)
            dve.wait_ge(consts_ready, 1)
            dve.wait_ge(pads_ready, 2)
            var0(Tile(0, 0))
            dve.wait_ge(w_both_in, 16)
            then(v.tensor_reduce(c_(WMAX), w_raw, AX.X, ALU.max, apply_absolute_value=True))
            then(v.tensor_scalar(c_(WMAX), c_(WMAX), W_FLOOR, None, ALU.max))
            then(v.tensor_scalar(c_(WPOW).bitcast(U32), c_(WMAX).bitcast(U32), 0x7F800000, None, ALU.bitwise_and))
            then(v.reciprocal(c_(WINV), c_(WPOW)))
            then(v.tensor_scalar(c_(WSC), c_(WINV), W_TOP, None, ALU.mult))
            then(v.tensor_scalar(c_(F_UP), c_(WINV), W_TOP * G_SCALE, None, ALU.mult))
            then(v.tensor_scalar(c_(G_UP), c_(WINV), W_TOP * G_SCALE * G_SCALE, None, ALU.mult))
            then(v.tensor_scalar(c_(G_DOWN), c_(WPOW), 1.0 / (W_TOP * G_SCALE), None, ALU.mult))
            v.tensor_scalar(c_(ROOT_DOWN), c_(G_DOWN), float(N_GROUP) ** 0.5, None, ALU.mult)
            then(v.tensor_scalar(bias[:], b_raw, c_(F_UP), None, ALU.mult))
            then(v.tensor_scalar(w_n, w_raw, c_(WSC), None, ALU.mult))
            w_n3 = w_n.rearrange("p (k i) -> p k i", k=KK)
            then(v.tensor_copy(dup_hi[:, :, 0, :], w_n3))
            then(v.tensor_copy(dup_hi[:, :, 1, :], dup_hi[:, :, 0, :]))
            then(v.tensor_tensor(dup_lo[:, :, 0, :], w_n3, dup_hi[:, :, 0, :], ALU.subtract))
            v.tensor_copy(dup_lo[:, :, 1, :], dup_lo[:, :, 0, :]).then_inc(dup_ready, 1)

            def copy_w():
                dve.wait_ge(w_turned, 1)
                for n, w in enumerate((w_hi, w_lo)):
                    wide = v.tensor_copy(w[:].rearrange("p k c -> p (k c)"), tap_ps[:, n, 0, :].bitcast(FP16)[:, 0:KK * C])
                wide.then_inc(w_copied, 1)

            def x1_linear(t, c):
                if c == 0:
                    dve.wait_ge(z_done, t.count(1, 1))
                dve.wait_ge(relu_done, t.count(CHUNKS, c + 1))
                xc = xb[:, t.slot, c * CH:(c + 1) * CH]
                v.scalar_tensor_tensor(xc, pw_ps[:, 0:CH], c_(C1_SG), xc, ALU.mult, ALU.add,
                                       accum_out=sums[:, t.par, 0, c:c + 1]).then_inc(y_done, 1)

            def centre_bias(t):
                wait_apart(dve, r1_step, t.count(1, 1))
                v.reciprocal(s_(t, INV1), s_(t, QS)).then_inc(inverse_done, 1)

            def low(t, half):
                dve.wait_ge(hi_done, t.count(2, half + 1))
                wait(dve, stacked[half], t.count(64))
                a, z = half * H // 2, (half + 1) * H // 2
                v.scalar_tensor_tensor(rows3(g_lo[:])[:, a:z, :], q[:, t.par, 1 + a:1 + z, 1:1 + WD], c_(G_UP),
                                       rows3(g_hi[:])[:, a:z, :], ALU.mult, ALU.subtract).then_inc(lo_done, 1)

            def product(t, u):
                qq, k = divmod(u, KK)
                n = PLACE[k]
                dy, dx = divmod(k, 3)
                if u == 0:
                    dve.wait_ge(q_done, t.count(1, 1))
                if u == 4:
                    dve.wait_ge(b4_done, t.count(1, 1))
                if k == 0:
                    wait(dve, folded, t.count(16 * 4, 16 * (qq - 1)))
                elif n in FREED:
                    wait(dve, added, t.count(4 * ADDS, ADDS * (qq - 2) + FREED[n]))
                dve.wait_ge(taps_ready, t.count(UNITS, u + 1))
                r = qq * QR + dy
                v.scalar_tensor_tensor(
                    prod[:, qq % 2, n, :].rearrange("p (j a b) -> p j a b", j=2, b=WD),
                    tap_ps[:, u % SLOTS, :, 0:CH].rearrange("p j (a b) -> p j a b", b=WD),
                    s_(t, B4) if k == 4 else bias[:, k:k + 1],
                    q[:, t.par, r:r + QR, dx:dx + WD].rearrange("p (j a) b -> p j a b", j=2),
                    ALU.add, ALU.mult).then_inc(prod_done, 1)

            def last_quarter(t):
                b_ = (QUARTERS - 1) % 2
                pr = prod[:, b_, :, :]
                dve.wait_ge(prod_done, t.count(UNITS, UNITS))
                v.tensor_tensor(pr[:, 0:4, :], pr[:, 0:4, :], pr[:, 4:8, :], ALU.add).then_inc(last_summed, 1)
                dve.wait_ge(last_summed, 1)
                v.tensor_tensor(pr[:, 0:2, :], pr[:, 0:2, :], pr[:, 2:4, :], ALU.add).then_inc(last_summed, 1)
                dve.wait_ge(last_summed, 2)
                v.tensor_tensor(pr[:, 0, :], pr[:, 0, :], pr[:, 1, :], ALU.add).then_inc(last_summed, 1)
                dve.wait_ge(last_summed, 3)
                dve.wait_ge(mean_added, t.count(4, QUARTERS))
                dve.wait_ge(stored[b_], t.count(16 * 2, 16))
                v.tensor_tensor(ob[:, b_, :], pr[:, 8, :], pr[:, 0, :], ALU.add).then_inc(last_summed, 1)

            def step(done, taps, mid, front, load):
                for u in range(UNITS):
                    if mid and mid.first and u == TURN_AT + 2:
                        copy_w()
                    for t, c in chunks_due(u, X1_DELAY, mid, front):
                        x1_linear(t, c)
                    if taps:
                        product(taps, u)
                    for at, who, what in ((MEAN0_AT, front, mean0), (VAR0_AT, front, var0), (MEAN1_AT, mid, mean1),
                                          (VAR1_AT, mid, var1), (B4_AT, mid, centre_bias)):
                        if u == at and who and not (who.first and what in (mean0, var0)):
                            what(who)
                    for half in range(2):
                        if mid and u == LOW_AT[half]:
                            low(mid, half)

            program(step, dve.Fori)
            last_quarter(Tile(0, TILES - 1))


FIRST_CHUNK = 13
CHUNK_EVERY = 4
PW_DELAY = 6
AB_DELAY = 2
X1_DELAY = 9
RELU_DELAY = 11
TURN_AT = 27
SUM0_AT = 1
MEAN0_AT = 1
SQUARE0_AT = 5
VAR0_AT = 7
R0_AT = 9
SIGN0_AT = 9
AFFINE0_AT = 14
SUM1_AT = 18
MEAN1_AT = 15
SQUARE1_AT = 18
VAR1_AT = 21
R1_AT = 23
Q_AT = 23
HI_AT = (28, 31)
B4_AT = 29
LOW_AT = (30, 34)
MEAN_DELAY = 2
ADD23_DELAY = 8
ADD01_DELAY = 9
ADD02_DELAY = 10
OUT_DELAY = 14
PLACE = (4, 5, 6, 7, 3, 1, 2, 0, 8)
FREED = {3: 1, 1: 2, 2: 3, 0: 4, 8: 4}

_INS = ["x", "L0_conv_dw_weight", "L0_conv_prelu1_a", "L0_conv_bn1_gamma", "L0_conv_bn1_beta", "L0_conv_bn1_mean",
        "L0_conv_bn1_var", "L0_conv_pw_weight", "L0_conv_prelu2_a", "L0_conv_bn2_gamma", "L0_conv_bn2_beta",
        "L0_conv_bn2_mean", "L0_conv_bn2_var", "L1_conv_W", "L1_conv_b"]


def kernel(**inputs):
    import numpy as _np
    import concourse.bacc as _bacc
    from concourse import mybir as _mybir
    from concourse.bass_utils import run_bass_kernel_spmd as _run

    nc = _bacc.Bacc("TRN2", target_bir_lowering=False, num_devices=1)
    arrays, args = {}, []
    for name in _INS:
        a = _np.ascontiguousarray(inputs[name])
        arrays[f"in_{name}_dram"] = a
        args.append(nc.dram_tensor(f"in_{name}_dram", a.shape, _mybir.dt.from_np(a.dtype), kind="ExternalInput").ap())
    shape = inputs["x"].shape
    args.append(nc.dram_tensor("out_0_dram", shape, _mybir.dt.from_np(_np.dtype("float32")), kind="ExternalOutput").ap())
    preact_involution_kernel(nc, *args)
    r = _run(nc, [arrays], core_ids=[0])
    return r.results[0]["out_0_dram"]
```
